# Optimizing a Trainium2 kernel written in Bass

```python
import numpy as np
import jax
import jax.numpy as jnp

def _softmax(x, axis=-1):
    return jax.nn.softmax(x, axis=axis)

def _gelu(x):
    return jax.nn.gelu(x, approximate=True)

def _silu(x):
    return jax.nn.silu(x)

def _sigmoid(x):
    return jax.nn.sigmoid(x)

def _layernorm(x, axis=-1, eps=1e-05):
    m = jnp.mean(x, axis=axis, keepdims=True)
    v = jnp.var(x, axis=axis, keepdims=True)
    return (x - m) / jnp.sqrt(v + eps)

def _scatter_add(tgt, idx, src, axis=0):
    return tgt.at[idx].add(src)

def _segment_sum(src, seg, n):
    return jax.ops.segment_sum(src, seg, n)
kernel_name = 'mk_adaln_d1_jaxref_r8_9622e4'

def setup_inputs(seed: int=0):
    np.random.seed(seed)
    _w = jnp.asarray

    def _L0_attn_setup():
        import jax, jax.numpy as jnp
        import numpy as np
        HEADS, HEAD_SIZE, FREQS, MAX_PERIOD = (16, 64, 32, 1250)
        D_MODEL = 128
        NEG_INF = -1000000000.0

        def sinusoid_embedding(seq_len, frequencies, max_period):
            pos = np.arange(seq_len, dtype=np.float64)[:, None]
            idx = np.arange(frequencies)[None, :]
            inv_freq = max_period ** (-(idx // 2 * 2) / frequencies)
            angle = pos * inv_freq
            table = np.where(idx % 2 == 0, np.sin(angle), np.cos(angle))
            return table.astype(np.float32)

        def relative_causal(scores):
            L = scores.shape[-1]
            d = jnp.clip(jnp.arange(L)[:, None] - jnp.arange(L)[None, :], 0, L - 1)
            return jnp.take_along_axis(scores, d[None, None, :, :], axis=-1)
        key = jax.random.key(seed)
        ks = jax.random.split(key, 4)
        u = np.sqrt(3.0)
        inp = jax.random.normal(ks[0], (2, 256, D_MODEL), dtype=jnp.float32)
        qkv = jax.random.uniform(ks[1], (D_MODEL, 3, HEADS, HEAD_SIZE), jnp.float32, -u, u)
        q_bias = jnp.zeros((HEADS, HEAD_SIZE), jnp.float32)
        positional = jax.random.uniform(ks[2], (FREQS, HEADS, HEAD_SIZE), jnp.float32, -u, u)
        out_kernel = jax.random.uniform(ks[3], (HEADS * HEAD_SIZE, D_MODEL), jnp.float32, -u, u)
        out_bias = jnp.zeros((D_MODEL,), jnp.float32)
        return {'input': inp, 'qkv': qkv, 'q_bias': q_bias, 'positional': positional, 'out_kernel': out_kernel, 'out_bias': out_bias}
    _L0_attn_in = _L0_attn_setup()

    def _L0_ffn_setup():
        import jax, jax.numpy as jnp
        import numpy as np
        B, S, D, H, E = (8, 256, 128, 512, 16)
        key = jax.random.key(seed)
        ks = jax.random.split(key, 4)
        sd = 1.0 / np.sqrt(D).astype(np.float32)
        sh = 1.0 / np.sqrt(H).astype(np.float32)
        return {'x': jax.random.normal(ks[0], (B, S, D), jnp.float32), 'Wg': jax.random.normal(ks[1], (D, E), jnp.float32) * sd, 'bg': jnp.zeros((E,), jnp.float32), 'W1': jax.random.normal(ks[2], (E, D, H), jnp.float32) * sd, 'b1': jnp.zeros((E, H), jnp.float32), 'W2': jax.random.normal(ks[3], (E, H, D), jnp.float32) * sh, 'b2': jnp.zeros((E, D), jnp.float32)}
    _L0_ffn_in = _L0_ffn_setup()
    _L0_c = _w((lambda *s: np.random.randn(*s).astype(np.float32) * 0.05)(8, 128))
    _L0_wmod = _w((lambda *s: np.random.randn(*s).astype(np.float32) * 0.05)(128, 6 * 128) * 128 ** (-0.5))
    _d = {'L0_attn_input': _L0_attn_in['input'], 'L0_attn_qkv': _L0_attn_in['qkv'], 'L0_attn_q_bias': _L0_attn_in['q_bias'], 'L0_attn_positional': _L0_attn_in['positional'], 'L0_attn_out_kernel': _L0_attn_in['out_kernel'], 'L0_attn_out_bias': _L0_attn_in['out_bias'], 'L0_ffn_Wg': _L0_ffn_in['Wg'], 'L0_ffn_bg': _L0_ffn_in['bg'], 'L0_ffn_W1': _L0_ffn_in['W1'], 'L0_ffn_b1': _L0_ffn_in['b1'], 'L0_ffn_W2': _L0_ffn_in['W2'], 'L0_ffn_b2': _L0_ffn_in['b2'], 'L0_c': _L0_c, 'L0_wmod': _L0_wmod}
    _x0 = _d['L0_attn_input']
    _d['L0_attn_input'] = jax.random.normal(jax.random.fold_in(jax.random.key(seed), 1), (8, 512, 128), dtype=_x0.dtype)
    del _x0
    return _d

def reference(L0_attn_input, L0_attn_qkv, L0_attn_q_bias, L0_attn_positional, L0_attn_out_kernel, L0_attn_out_bias, L0_ffn_Wg, L0_ffn_bg, L0_ffn_W1, L0_ffn_b1, L0_ffn_W2, L0_ffn_b2, L0_c, L0_wmod):

    def _L0_attn_ref(input, qkv, q_bias, positional, out_kernel, out_bias):
        import jax, jax.numpy as jnp
        import numpy as np
        HEADS, HEAD_SIZE, FREQS, MAX_PERIOD = (16, 64, 32, 1250)
        D_MODEL = 128
        NEG_INF = -1000000000.0

        def sinusoid_embedding(seq_len, frequencies, max_period):
            pos = np.arange(seq_len, dtype=np.float64)[:, None]
            idx = np.arange(frequencies)[None, :]
            inv_freq = max_period ** (-(idx // 2 * 2) / frequencies)
            angle = pos * inv_freq
            table = np.where(idx % 2 == 0, np.sin(angle), np.cos(angle))
            return table.astype(np.float32)

        def relative_causal(scores):
            L = scores.shape[-1]
            d = jnp.clip(jnp.arange(L)[:, None] - jnp.arange(L)[None, :], 0, L - 1)
            return jnp.take_along_axis(scores, d[None, None, :, :], axis=-1)
        b, s, x = input.shape
        n, h = (HEADS, HEAD_SIZE)
        w = qkv * (3.0 * x * h * n) ** (-0.25)
        q, k, v = jnp.einsum('bsx,xAnh->Abnsh', input, w)
        q = q + q_bias[:, None, :]
        a = jnp.einsum('bnqh,bnkh->bnqk', q, k) * h ** (-0.5)
        sins = jnp.asarray(np.sqrt(2.0) * sinusoid_embedding(s, FREQS, MAX_PERIOD))
        emb = jnp.einsum('sf,fnh->nsh', sins, positional * FREQS ** (-0.5))
        pos_scores = jnp.einsum('bnqh,nvh->bnqv', q, emb) * h ** (-0.5)
        a = a + relative_causal(pos_scores)
        mask = jnp.tril(jnp.ones((s, s), dtype=bool))
        a = jax.nn.softmax(jnp.where(mask, a, NEG_INF), axis=-1)
        o = jnp.einsum('bnqk,bnkh->bqnh', a, v).reshape(b, s, n * h)
        fan_in, fan_out = out_kernel.shape
        out = o @ (out_kernel * (fan_in * fan_out) ** (-0.25)) + out_bias
        return out

    def _L0_ffn_ref(x, Wg, bg, W1, b1, W2, b2):
        import jax, jax.numpy as jnp
        import numpy as np
        B, S, D, H, E = (8, 256, 128, 512, 16)
        d = x.shape[-1]
        xf = x.reshape(-1, d)
        n_tok = xf.shape[0]
        n_exp = Wg.shape[1]
        cap = -(-n_tok // n_exp)
        score = jax.nn.softmax(xf @ Wg + bg, axis=-1)
        gate = jnp.max(score, axis=-1)
        idx = jnp.argmax(score, axis=-1)
        onehot = jax.nn.one_hot(idx, n_exp, dtype=jnp.int32)
        pos = jnp.sum((jnp.cumsum(onehot, axis=0) - 1) * onehot, axis=-1)
        keep = pos < cap
        safe_pos = jnp.where(keep, pos, cap - 1)
        buf = jnp.zeros((n_exp, cap, d), x.dtype).at[idx, safe_pos].add(jnp.where(keep[:, None], xf, 0.0))
        h = jax.nn.relu(jnp.einsum('ecd,edh->ech', buf, W1) + b1[:, None, :])
        y = jnp.einsum('ech,ehd->ecd', h, W2) + b2[:, None, :]
        out = y[idx, safe_pos] * gate[:, None]
        out = jnp.where(keep[:, None], out, 0.0)
        return out.reshape(x.shape)
    x = L0_attn_input
    mod = (_silu(L0_c) @ L0_wmod).reshape(L0_c.shape[0], 6, 1, -1)
    sa, ca, ga, sb, cb, gb = (mod[:, 0], mod[:, 1], mod[:, 2], mod[:, 3], mod[:, 4], mod[:, 5])
    ga = (2 * (ga >= 0) - 1) * jnp.maximum(jnp.abs(ga), 0.25)
    gb = (2 * (gb >= 0) - 1) * jnp.maximum(jnp.abs(gb), 0.25)
    h = _layernorm(x, axis=-1) * (1 + ca) + sa
    x = x + ga * _L0_attn_ref(h, L0_attn_qkv, L0_attn_q_bias, L0_attn_positional, L0_attn_out_kernel, L0_attn_out_bias)
    h = _layernorm(x, axis=-1) * (1 + cb) + sb
    x = x + gb * _L0_ffn_ref(h, L0_ffn_Wg, L0_ffn_bg, L0_ffn_W1, L0_ffn_b1, L0_ffn_W2, L0_ffn_b2)
    return x

_drawn_inputs = setup_inputs


def setup_inputs(seed=0):
    import zlib

    import numpy as np

    out = dict(_drawn_inputs(seed))
    spreads = {'L0_attn_q_bias': (0.0, 0.8),
     'L0_attn_out_bias': (0.0, 0.32),
     'L0_ffn_bg': (0.0, 0.466),
     'L0_ffn_b1': (0.0, 0.8),
     'L0_ffn_b2': (0.0, 0.8)}
    factors = {'L0_attn_positional': 8.0}
    for name, (base, spread) in spreads.items():
        noise = np.random.default_rng([zlib.crc32(name.encode()), seed]).standard_normal(out[name].shape)
        drawn = base * np.exp(spread * noise) if base else spread * noise
        out[name] = jnp.asarray(drawn.astype(out[name].dtype))
    for name, factor in factors.items():
        out[name] = (out[name] * factor).astype(out[name].dtype)
    return out
```

```python
from contextlib import ExitStack

import numpy as np
import concourse.bass as bass
from concourse import mybir

F32 = mybir.dt.float32
BF16 = mybir.dt.bfloat16
U32 = mybir.dt.uint32
ALU = mybir.AluOpType
ACT = mybir.ActivationFunctionType
AX = mybir.AxisListType

P = 128
B, S, D = 8, 512, 128
HEADS, HD, FREQS = 16, 64, 32
PAIRS = HEADS // 2
NJ = B * PAIRS
TILES = B * S // P
QT = S // P
E, FF = 16, 512
CAP = B * S // E
NB = FF // P
ST = CAP // P
EPS = 1e-5
C_QKV = (3.0 * D * HD * HEADS) ** -0.25
C_OUT = (HEADS * HD * D) ** -0.25
NEG = -1e30
BIG = 3e38
WP = 2 * P + P + 2
GW = [S, 384, 384]
GROUPS = [[(q, 0) for q in range(4)], [(q, 1) for q in range(1, 4)], [(2, 2), (3, 2), (3, 3)]]
QOFF = [0, 128, 384, 768]
KOFF = [0, 512, 896, 1152]
PW = 1280
TURN = [0, 1, 2, 3, 4, 5]
ORDER = [3, 2, 1, 0]


def program(nc, x_d, qkv_d, qb_d, pos_d, wo_d, bo_d, wg_d, bg_d, w1_d, b1_d, w2_d, b2_d, c_d, wmod_d,
            consts_d, ktab_d, out_d):
    ctx = ExitStack()
    with ctx:
        def sb(name, shape, dt=F32):
            return ctx.enter_context(nc.sbuf_tensor(name, shape, dt))

        def sem(name):
            return ctx.enter_context(nc.semaphore(name))

        x = sb("x", [P, TILES, D])
        acc = sb("acc", [P, TILES, D])
        hT = sb("hT_all", [P, B * S])
        modb = sb("modb", [P, B, 4, D])
        wall = sb("wall", [P, PAIRS, WP])
        qkv = sb("qkv", [P, 3, HEADS * HD])
        wo = sb("wo", [P, PAIRS, D])
        wmod = sb("wmod", [P, 6, D])
        consts = sb("consts", [P, 128 + 512 + 512 + 16 + 128])
        ident = consts[:, 0:128]
        mask = consts[:, 128:640]
        qtab = consts[:, 640:1152]
        desc = consts[:, 1152:1168]
        upper = consts[:, 1168:1296]
        small = sb("small", [80, P])
        smallT = sb("smallT", [P, 80])
        pos = sb("pos", [FREQS, HEADS * HD])
        posT = sb("posT", [P, PAIRS, 2, FREQS])
        wg = sb("wg", [P, E])
        bg = sb("bg", [P, E])
        b2 = sb("b2", [P, E, D])
        silu = sb("silu", [P, 4, B])
        modT = sb("modT", [P, 2, B])
        stats = sb("stats", [P, TILES, 6])
        mom = sb("mom", [P, 6, TILES])
        xn = sb("xn", [P, 2, QT, D])
        mhalf = sb("mhalf", [P, TILES])
        upper16 = sb("upper16", [P, P], BF16)
        ones16 = sb("ones16", [P, P], BF16)
        wq = sb("wq", [P, 2, WP])
        hTb = sb("hTb", [P, S])
        qx = sb("qx", [P, 2, S])
        kx = sb("kx", [P, 2, S])
        v = sb("v", [P, 2, QT, P])
        srow = sb("srow", [P, 4, S])
        nmax = sb("nmax", [P, 2, 8])
        sums = sb("sums", [P, 2, 8])
        rsum = sb("rsum", [P, 2, 8])
        prob = sb("prob", [P, 2, 2, PW])
        pt = sb("pt", [P, 2, PW])
        oT = sb("oT", [P, S])
        zeros = srow[:, 0, :]
        ptf = pt[:, :, :].rearrange("p a w -> p (a w)")
        rt = [ptf[:, i * 512:(i + 1) * 512] for i in range(4)]
        lgt = ptf[:, 2048:2560]
        oh16 = sb("oh16", [P, TILES * E], BF16)
        rsm = sb("rsm", [P, 10, TILES])
        sidx = sb("sidx", [P, TILES], U32)
        gidx = sb("gidx", [P, TILES], U32)
        reset = sb("reset", [P, E, TILES])
        hst = v
        hid = acc[:, :, :].rearrange("p t d -> p (t d)")[:, 0:2 * NB * CAP].rearrange("p (a n c) -> p a n c", a=2, n=NB)
        bank = [ctx.enter_context(nc.psum_tensor(f"bank{i}", [P, 512], F32)) for i in range(8)]
        scb, trb, prb, otb, opb = bank[0:2], bank[2:4], bank[4:6], bank[6], bank[7]
        xbuf = nc.dram_tensor("xbuf", [E * CAP, D], F32).ap()
        ybuf = nc.dram_tensor("ybuf", [E * CAP, D], F32).ap()

        names = ("consts ktab small pos qkv x0 x1 wmod misc wo zero zfill "
                 "t_small smallT e_silu silu t_pos posT t_wq wqT wg_mm wall mod_mm modT bc_mm modb "
                 "rst rs1 xn1 t_x hT accz mm0 "
                 "sc tt ex rc nm tr evA evB pv oe qp qe kp ke vp ve op ac wld0 wld1 hld "
                 "dch ach pch hh2 x2 rs2 xh h2a h2 t_h hh lg lge oh pre idx scat sdma "
                 "xl0 xl1 w0 w1 w2 w3 tx xt hm hr ym ye ys0 ys1 outd fin "
                 "gat0 gat1 gat2 gat3 gat4 gat5 gat6 gat7").split()
        s = {n: sem("s_" + n) for n in names}

        class Chain:

            def __init__(self, eng, semaphore):
                self.eng, self.sem, self.n = eng, semaphore, 0

            def __call__(self, ins):
                self.n += 1
                ins.then_inc(self.sem, 1)
                self.eng.wait_ge(self.sem, self.n)

        def wait(eng, name, value):
            if not isinstance(value, int) or value > 0:
                eng.wait_ge(s[name], value)

        def waits(eng, *pairs):
            values = [v if isinstance(v, int) else eng.compute_val(v) for _, v in pairs]
            for (name, _), v in zip(pairs, values):
                wait(eng, name, v)

        block = ctx.enter_context(nc.Block())

        @block.sync
        def _(sp):
            sp.dma_start(consts[:, :], consts_d).then_inc(s["consts"], 16)
            sp.dma_start(small[0:8, :], qb_d.rearrange("(a h) d -> a (h d)", h=2)).then_inc(s["small"], 16)
            sp.dma_start(small[8:16, :], c_d).then_inc(s["small"], 16)
            sp.dma_start(small[16:80, :], b1_d.rearrange("e (n p) -> (e n) p", p=P)).then_inc(s["small"], 16)
            sp.dma_start(wmod[:, :, :], wmod_d.rearrange("p (a b) -> p a b", a=6)).then_inc(s["wmod"], 16)
            xt_d = x_d.rearrange("b (t p) d -> p (b t) d", p=P)
            for h in range(2):
                sp.dma_start(x[:, h * 16:(h + 1) * 16, :], xt_d[:, h * 16:(h + 1) * 16, :]).then_inc(s[f"x{h}"], 16)
            sp.dma_start(wo[:, :, :], wo_d.rearrange("(a p) d -> p a d", p=P)).then_inc(s["wo"], 16)
            sp.wait_ge(s["zero"], 1)
            for q in range(8):
                sp.dma_start(xbuf.rearrange("(p r) d -> p (r d)", p=P)[:, q * 512:(q + 1) * 512],
                             zeros).then_inc(s["zfill"], 16)
            sp.wait_ge(s["wall"], 7)
            for j in range(2):
                sp.dma_start(wq[:, j, :], wall[:, j, :]).then_inc(s[f"wld{j}"], 16)
            sp.wait_ge(s["hT"], 8)
            sp.dma_start(hTb[:, :], hT[:, 0:S]).then_inc(s["hld"], 16)

            def at(value):
                return value if isinstance(value, int) else sp.compute_val(value)

            def step(j, even_next):
                pair = at(((j + 2) & 7) * WP)
                waits(sp, ("wall", 7), ("qe", 2 * j + 2), ("ke", 2 * j + 2))
                par = 1 if even_next else 0
                sp.dma_start(wq[:, par, :], wall[:, :, :].rearrange("p a w -> p (a w)")[:, bass.ds(pair, WP)])\
                    .then_inc(s[f"wld{par}"], 16)
                if even_next:
                    row = at((((j + 1) >> 3) & 7) * S)
                    waits(sp, ("hT", B), ("vp", j + 1))
                    sp.dma_start(hTb[:, :], hT[:, bass.ds(row, S)]).then_inc(s["hld"], 16)

            step(0, False)
            with sp.Fori(0, NJ // 2 - 1) as t:
                step(2 * t + 1, True)
                step(2 * t + 2, False)

            sp.wait_ge(s["pv"], NJ)
            wring = prob[:, :, :, :].rearrange("p a b w -> p (a b w)")

            def weights(e, slot):
                e = at(e)
                sp.dma_start(wring[:, slot * 1024:slot * 1024 + 512],
                             w1_d[bass.ds(e, 1), :, :].rearrange("a p n -> p (a n)")).then_inc(s[f"w{slot}"], 16)
                sp.dma_start(wring[:, slot * 1024 + 512:slot * 1024 + 1024].rearrange("p (n d) -> p n d", n=NB),
                             w2_d[bass.ds(e, 1), :, :].rearrange("a (n p) d -> p (a n) d", p=P))\
                    .then_inc(s[f"w{slot}"], 16)

            def rows(e, slot):
                sp.dma_start(xn[:, slot, 0:ST, :],
                             xbuf.rearrange("(e t p) d -> e p t d", p=P, t=ST)[bass.ds(e, 1), :, :, :]
                             .rearrange("a p t d -> p (a t) d")).then_inc(s[f"xl{slot}"], 16)

            def yout(e, slot):
                sp.wait_ge(s["ye"], e + 3)
                sp.dma_start(ybuf.rearrange("(e t p) d -> e p t d", p=P, t=ST)[bass.ds(e, 1), :, :, :]
                             .rearrange("a p t d -> p (a t) d"), xn[:, slot, 2:4, :]).then_inc(s[f"ys{slot}"], 16)

            for e in range(4):
                weights(e, e)
            sp.wait_ge(s["scat"], 16 * TILES)
            for e in range(2):
                rows(e, e)
            with sp.Fori(0, E // 4 - 1) as g:
                for r in range(4):
                    e = 4 * g + r
                    sp.wait_ge(s["tx"], e + 1)
                    rows(e + 2, r % 2)
                    yout(e, r % 2)
                    sp.wait_ge(s["ym"], e + 1)
                    weights(e + 4, r)
            for e in range(E - 4, E):
                if e + 2 < E:
                    sp.wait_ge(s["tx"], e + 1)
                    rows(e + 2, e % 2)
                yout(e, e % 2)
            out_v = out_d.rearrange("b (t p) d -> p b t d", p=P)
            for b in range(B):
                sp.wait_ge(s["fin"], b + 1)
                sp.dma_start(out_v[:, b, :, :], x[:, b * QT:(b + 1) * QT, :]).then_inc(s["outd"], 16)
            sp.wait_ge(s["outd"], 16 * B)
            sp.wait_ge(s["zfill"], 128)
            sp.wait_ge(s["ys0"], 8 * E)
            sp.wait_ge(s["ys1"], 8 * E)

        @block.gpsimd
        def _(gp):
            gp.memset(mhalf[:, :], -0.5).then_inc(s["pch"], 1)
            gp.wait_ge(s["pch"], 1)
            gp.wait_ge(s["qkv"], 16)
            for h in range(2):
                gp.tensor_copy(wall[:, :, h * P:h * P + HD],
                               qkv[:, 0, :].rearrange("p (a h d) -> p a h d", h=2, d=HD)[:, :, h, :])\
                    .then_inc(s["wall"], 1)
            gp.tensor_copy(wall[:, :, 2 * P:3 * P], qkv[:, 1, :].rearrange("p (a w) -> p a w", a=PAIRS))\
                .then_inc(s["wall"], 1)
            gp.wait_ge(s["rst"], 1)
            gp.tensor_tensor(mom[:, 5, :], mom[:, 4, :], mhalf[:, :], ALU.pow).then_inc(s["rs1"], 1)

            def step(j, par):
                for h in range(2):
                    waits(gp, ("rs1", 1), ("rc", 2 * j + h + 1))
                    for q in range(QT):
                        row = prob[:, par, h, QOFF[q]:QOFF[q] + P * (q + 1)]
                        last = gp.tensor_scalar(row, row, rsum[:, par, 4 * h + q:4 * h + q + 1], 1.0,
                                                ALU.mult, ALU.mult)
                    last.then_inc(s["nm"], 1)

            step(0, 0)
            with gp.Fori(0, NJ // 2 - 1) as t:
                step(2 * t + 1, 1)
                step(2 * t + 2, 0)
            step(NJ - 1, 1)

            gp.wait_ge(s["rst"], 2)
            gp.tensor_tensor(mom[:, 5, :], mom[:, 4, :], mhalf[:, :], ALU.pow).then_inc(s["rs2"], 1)
            with gp.Fori(0, B) as b:
                gp.wait_ge(s["h2a"], b + 1)
                hb = acc[:, bass.ds(b * QT, QT), :]
                gp.tensor_tensor(hb, hb, modb[:, bass.ds(b, 1), 1, :].to_broadcast([P, QT, D]), ALU.add)\
                    .then_inc(s["h2"], 1)
            gp.wait_ge(s["idx"], 1)
            gp.wait_ge(s["zfill"], 128)
            gp.wait_ge(s["h2"], B)
            for t in range(TILES):
                gp.indirect_dma_start(out=xbuf, out_offset=bass.IndirectOffsetOnAxis(ap=sidx[:, t:t + 1], axis=0),
                                      in_=acc[:, t, :], in_offset=None,
                                      bounds_check=E * CAP - 1, oob_is_err=False).then_inc(s["scat"], 16)
            gp.wait_ge(s["ys0"], 8 * E)
            gp.wait_ge(s["ys1"], 8 * E)
            yg = hT[:, :].rearrange("p (t d) -> p t d", d=D)
            for t in range(TILES):
                gp.indirect_dma_start(out=yg[:, t, :], out_offset=None, in_=ybuf,
                                      in_offset=bass.IndirectOffsetOnAxis(ap=gidx[:, t:t + 1], axis=0))\
                    .then_inc(s[f"gat{t // QT}"], 16)

        @block.scalar
        def _(act):
            act.dma_start(pos[:, :], pos_d.rearrange("f n d -> f (n d)")).then_inc(s["pos"], 16)
            act.dma_start(qkv[:, :, :], qkv_d.rearrange("p a n d -> p a (n d)")).then_inc(s["qkv"], 16)
            for h in range(2):
                act.dma_start(kx[HD:P, h, :], ktab_d).then_inc(s["ktab"], 16)
            act.dma_start(wg[:, :], wg_d).then_inc(s["misc"], 16)
            act.dma_start(bg[:, :], bg_d.rearrange("(a n) -> a n", a=1).to_broadcast([P, E])).then_inc(s["misc"], 16)
            act.dma_start(b2[:, :, :], b2_d.rearrange("(a e) d -> a e d", a=1).to_broadcast([P, E, D]))\
                .then_inc(s["misc"], 16)
            act.dma_start(oT[:, 0:D], bo_d.rearrange("(a n) -> a n", a=1).to_broadcast([P, D]))\
                .then_inc(s["misc"], 16)
            act.wait_ge(s["smallT"], 1)
            act.activation(silu[:, 0, :], smallT[:, 8:16], ACT.Exp, scale=-1.0).then_inc(s["e_silu"], 1)
            act.wait_ge(s["wg_mm"], 1)
            for h in range(2):
                act.activation(wall[:, :, h * P + HD:(h + 1) * P], bank[4 + h][:, :].rearrange("p (a w) -> p a w", a=PAIRS),
                               ACT.Copy).then_inc(s["wall"], 1)
            act.wait_ge(s["wg_mm"], 2)
            for h in range(2):
                act.activation(wall[HD:P, :, 3 * P + h], bank[6 + h][HD:P, 0:PAIRS], ACT.Copy, scale=1.0 / C_QKV)\
                    .then_inc(s["ach"], 1)
                last = act.activation(wall[0:HD, :, 3 * P + h], smallT[h * HD:(h + 1) * HD, 0:PAIRS], ACT.Copy,
                                      scale=1.0 / C_QKV)
                last.then_inc(s["wall"], 1)
            act.wait_ge(s["ach"], 2)
            act.wait_ge(s["misc"], 64)
            act.activation(acc[:, :, :], oT[:, None, 0:D].to_broadcast([P, TILES, D]), ACT.Copy)\
                .then_inc(s["accz"], 1)
            act.wait_ge(s["modT"], 2)
            with act.Fori(0, B // 2) as t:
                for r in range(2):
                    b = 2 * t + r
                    act.wait_ge(s["t_x"], b + 1)
                    act.activation(hT[:, bass.ds(b * S, S)], bank[r][:, :], ACT.Identity,
                                   bias=modT[:, 0, bass.ds(b, 1)], scale=modT[:, 1, bass.ds(b, 1)])\
                        .then_inc(s["hT"], 1)

            def evac_k(j, h):
                act.wait_ge(s["kp"], j + 1)
                act.activation(kx[0:HD, h, :], prb[0][h * HD:(h + 1) * HD, :], ACT.Copy, scale=C_QKV)\
                    .then_inc(s["ke"], 1)

            def evac_v(j, par):
                act.wait_ge(s["vp"], j + 1)
                act.activation(v[:, par, :, :], prb[1][:, :].rearrange("p (t w) -> p t w", t=QT), ACT.Copy)\
                    .then_inc(s["ve"], 1)

            def exps(j, par, k):
                h, q = k // QT, ORDER[k % QT]
                act.wait_ge(s["tt"], 8 * j + k + 1)
                act.activation(prob[:, par, h, QOFF[q]:QOFF[q] + P * (q + 1)], srow[:, k % 4, 0:P * (q + 1)],
                               ACT.Exp, bias=nmax[:, par, k:k + 1], scale=-1.0,
                               accum_out=sums[:, par, 4 * h + q:4 * h + q + 1]).then_inc(s["ex"], 1)

            def evac_pt(j, g):
                act.wait_ge(s["tr"], 6 * j + 3 + g + 1)
                act.activation(pt[:, 1, KOFF[g]:KOFF[g] + GW[g]], trb[(3 + g) % 2][:, 0:GW[g]], ACT.Copy)\
                    .then_inc(s["evB"], 1)

            def evac_o(j):
                act.wait_ge(s["pv"], j + 1)
                act.activation(oT[:, :], otb[:, :], ACT.Copy, scale=C_QKV * C_OUT).then_inc(s["oe"], 1)

            def step(j, par, before=True, after=True):
                for k in range(8):
                    if before and k == 5:
                        evac_pt(j - 1, 2)
                    exps(j, par, k)
                    if k == 1:
                        evac_v(j, par)
                    if before and 3 <= k < 5:
                        evac_pt(j - 1, k - 3)
                    if after and k == 5:
                        evac_k(j + 1, 0)
                    if before and k == 6:
                        evac_o(j - 1)
                if after:
                    evac_k(j + 1, 1)

            for h in range(2):
                evac_k(0, h)
            step(0, 0, before=False)
            with act.Fori(0, NJ // 2 - 1) as t:
                step(2 * t + 1, 1)
                step(2 * t + 2, 0)
            step(NJ - 1, 1, after=False)
            for g in range(3):
                evac_pt(NJ - 1, g)
            evac_o(NJ - 1)

            act.wait_ge(s["x2"], B + 1)
            with act.Fori(0, B) as b:
                for q in range(QT):
                    t = b * QT + q
                    last = act.activation(acc[:, bass.ds(t, 1), :].rearrange("p a d -> p (a d)"),
                                          x[:, bass.ds(t, 1), :].rearrange("p a d -> p (a d)"), ACT.Identity,
                                          bias=mom[:, 0, bass.ds(t, 1)], scale=mom[:, 5, bass.ds(t, 1)])
                last.then_inc(s["xh"], 1)
            with act.Fori(0, B // 2) as t:
                for r in range(2):
                    b = 2 * t + r
                    act.wait_ge(s["t_h"], b + 1)
                    act.activation(xn[:, r, :, :], bank[r][:, :].rearrange("p (t d) -> p t d", t=QT), ACT.Copy)\
                        .then_inc(s["hh"], 1)
            act.wait_ge(s["lge"], B + 1)
            act.activation(rt[1], rt[0], ACT.Exp).then_inc(s["lge"], 1)

            def expert(e, par):
                act.wait_ge(s["tx"], e + 1)
                act.activation(qx[:, par, 0:CAP], bank[par][:, 0:CAP], ACT.Copy).then_inc(s["xt"], 1)
                for n in range(0, NB, 2):
                    act.wait_ge(s["hm"], NB * e + n + 1)
                    act.activation(hid[:, par, n, :], bank[2 + n][:, 0:CAP], ACT.Relu,
                                   bias=smallT[:, bass.ds(16 + NB * e + n, 1)]).then_inc(s["hr"], 1)

            with act.Fori(0, E // 2) as g:
                expert(2 * g, 0)
                expert(2 * g + 1, 1)

        @block.tensor
        def _(pe):
            pe.wait_ge(s["consts"], 16)
            pe.wait_ge(s["small"], 48)
            pe.transpose(bank[0][:, 0:80], small[:, :], ident[0:80, 0:80]).then_inc(s["t_small"], 1)
            pe.wait_ge(s["pos"], 16)
            for a in range(PAIRS):
                last = pe.transpose(bank[1][:, a * FREQS:(a + 1) * FREQS], pos[:, a * P:(a + 1) * P],
                                    ident[0:FREQS, 0:FREQS])
            last.then_inc(s["t_pos"], 1)
            pe.wait_ge(s["qkv"], 16)
            for a in range(PAIRS):
                last = pe.transpose(bank[2 + a // 4][:, (a % 4) * P:(a % 4 + 1) * P], qkv[:, 0, a * P:(a + 1) * P],
                                    ident)
                if a % 4 == 3:
                    last.then_inc(s["t_wq"], 1)
            wqT = prob[:, 0, :, :].rearrange("p a w -> p (a w)")[:, 0:PAIRS * P]
            pe.wait_ge(s["posT"], 2)
            pe.wait_ge(s["wqT"], 2)
            for h in range(2):
                for a in range(PAIRS):
                    last = pe.matmul(bank[4 + h][:, a * 64:(a + 1) * 64], wqT[h * HD:(h + 1) * HD, a * P:(a + 1) * P],
                                     posT[h * HD:(h + 1) * HD, a, :, :].rearrange("p a f -> p (a f)"),
                                     start=True, stop=True)
            last.then_inc(s["wg_mm"], 1)
            pe.wait_ge(s["smallT"], 1)
            for h in range(2):
                for a in range(PAIRS):
                    last = pe.matmul(bank[6 + h][HD:P, a:a + 1],
                                     posT[h * HD:(h + 1) * HD, a, :, :].rearrange("p a f -> p (a f)"),
                                     smallT[h * HD:(h + 1) * HD, a:a + 1], start=True, stop=True)
            last.then_inc(s["wg_mm"], 1)
            pe.wait_ge(s["silu"], 2)
            pe.wait_ge(s["wmod"], 16)
            for i in range(2):
                last = pe.matmul(bank[0][:, i * B:(i + 1) * B], wmod[:, i, :], silu[:, 3, :], start=True, stop=True)
            last.then_inc(s["mod_mm"], 1)
            sbc = prob[:, 1, :, :].rearrange("p a w -> p (a w)")[:, 0:B * P]
            for b in range(B):
                if b >= 2:
                    pe.wait_ge(s["modb"], b - 1)
                pe.matmul(bank[2 + b % 2][:, :], sbc[:, b * P:(b + 1) * P],
                          wmod[:, 2:6, :].rearrange("p a d -> p (a d)"), start=True, stop=True)\
                    .then_inc(s["bc_mm"], 1)
            pe.wait_ge(s["modT"], 2)
            with pe.Fori(0, B // 2) as t:
                for r in range(2):
                    b = 2 * t + r
                    pe.wait_ge(s["xn1"], b + 1)
                    if r == 0:
                        pe.wait_ge(s["hT"], b)
                    for q in range(QT):
                        last = pe.transpose(bank[r][:, q * P:(q + 1) * P], xn[:, r, q, :], ident)
                    last.then_inc(s["t_x"], 1)

            def rows_of(j):
                return hT[:, bass.ds(((j >> 3) & 7) * S, S)]

            def project_q(j, par, h):
                if h == 0:
                    pe.wait_ge(s[f"wld{par}"], 8 * (j - par) + 16)
                else:
                    wait(pe, "ve", j)
                pe.matmul(prb[h][:, :], wq[:, par, h * P:(h + 1) * P], rows_of(j), start=True, stop=True)\
                    .then_inc(s["qp"], 1)

            def project_k(j, par):
                pe.wait_ge(s["qe"], 2 * j + 1)
                pe.matmul(prb[0][:, :], wq[:, par, 2 * P:3 * P], rows_of(j), start=True, stop=True)\
                    .then_inc(s["kp"], 1)

            def project_v(j, par, pair):
                if par == 0:
                    pe.wait_ge(s["hld"], 8 * j + 16)
                pe.wait_ge(s["qe"], 2 * j + 2)
                for t in range(QT):
                    last = pe.matmul(prb[1][:, t * P:(t + 1) * P], hTb[:, t * P:(t + 1) * P],
                                     qkv[:, 2, bass.ds(pair * P, P)], start=True, stop=True)
                last.then_inc(s["vp"], 1)

            def scores(j, k):
                h, q = k // QT, ORDER[k % QT]
                if k % QT == 0:
                    pe.wait_ge(s["qe"], 2 * j + h + 1)
                    pe.wait_ge(s["ke"], 2 * j + h + 1)
                wait(pe, "tt", 8 * j + k - 1)
                pe.matmul(scb[k % 2][:, 0:P * (q + 1)], qx[:, h, q * P:(q + 1) * P], kx[:, h, 0:P * (q + 1)],
                          start=True, stop=True).then_inc(s["sc"], 1)

            def transposes(j, par, h, g):
                if g == 0:
                    pe.wait_ge(s["nm"], 2 * j + h + 1)
                i = 3 * h + g
                if i >= 2:
                    n = i - 2
                    pe.wait_ge(s["evB" if n >= 3 else "evA"], 3 * j + n % 3 + 1)
                for n, (q, k) in enumerate(GROUPS[g]):
                    last = pe.transpose(trb[i % 2][:, n * P:(n + 1) * P],
                                        prob[:, par, h, QOFF[q] + k * P:QOFF[q] + (k + 1) * P], ident)
                last.then_inc(s["tr"], 1)

            def weighted(j, par):
                pe.wait_ge(s["evA"], 3 * j + 3)
                pe.wait_ge(s["evB"], 3 * j + 3)
                pe.wait_ge(s["ve"], j + 1)
                wait(pe, "oe", j)
                for k in range(QT):
                    for h in range(2):
                        last = pe.matmul(otb[h * HD:(h + 1) * HD, k * P:S], v[:, par, k, h * HD:(h + 1) * HD],
                                         pt[:, h, KOFF[k]:KOFF[k] + S - k * P], start=(k == 0), stop=(k == QT - 1))
                last.then_inc(s["pv"], 1)

            def project_out(j, pair):
                pe.wait_ge(s["oe"], j + 1)
                wait(pe, "ac", j)
                for t in range(QT):
                    last = pe.matmul(opb[:, t * P:(t + 1) * P], oT[:, t * P:(t + 1) * P],
                                     wo[:, bass.ds(pair, 1), :].rearrange("p a d -> p (a d)"),
                                     start=True, stop=True)
                last.then_inc(s["op"], 1)

            def step(j, par, before=True, after=True):
                for k in range(8):
                    scores(j, k)
                    if k == 4 and after:
                        project_q(j + 1, 1 - par, 0)
                    if before and k in TURN:
                        transposes(j - 1, 1 - par, *divmod(TURN.index(k), 3))
                    if k == 1:
                        project_v(j, par, j & 7)
                    if k == 5 and after:
                        project_k(j + 1, 1 - par)
                    if k == 6 and before:
                        weighted(j - 1, 1 - par)
                if after:
                    project_q(j + 1, 1 - par, 1)
                if before:
                    project_out(j - 1, (j - 1) & 7)

            pe.wait_ge(s["wo"], 16)
            project_q(0, 0, 0)
            project_q(0, 0, 1)
            project_k(0, 0)
            pe.wait_ge(s["ktab"], 32)
            step(0, 0, before=False)
            with pe.Fori(0, NJ // 2 - 1) as t:
                step(2 * t + 1, 1)
                step(2 * t + 2, 0)
            step(NJ - 1, 1, after=False)
            for h in range(2):
                for g in range(3):
                    transposes(NJ - 1, 1, h, g)
            weighted(NJ - 1, 1)
            project_out(NJ - 1, PAIRS - 1)

            pe.wait_ge(s["misc"], 64)
            with pe.Fori(0, B // 2) as t:
                for r in range(2):
                    b = 2 * t + r
                    pe.wait_ge(s["h2a"], B + b + 1)
                    for q in range(QT):
                        last = pe.transpose(bank[r][:, q * P:(q + 1) * P], hst[:, r, q, :], ident)
                    last.then_inc(s["t_h"], 1)
                    pe.wait_ge(s["hh"], b + 1)
                    pe.wait_ge(s["lge"], b)
                    for q in range(QT):
                        last = pe.matmul(bank[2][:, q * E:(q + 1) * E], xn[:, r, q, :], wg[:, :], start=True, stop=True)
                    last.then_inc(s["lg"], 1)
            pe.wait_ge(s["oh"], 1)
            pe.matmul(bank[3][:, :], upper16[:, :], oh16[:, :], start=True, stop=True)
            pe.matmul(bank[4][:, :], ones16[:, :], oh16[:, :], start=True, stop=True).then_inc(s["pre"], 1)

            wring = prob[:, :, :, :].rearrange("p a b w -> p (a b w)")

            def turn(e, slot):
                for t in range(ST):
                    last = pe.transpose(bank[slot][:, t * P:(t + 1) * P], xn[:, slot, t, :], ident)
                last.then_inc(s["tx"], 1)

            def hidden(e, r):
                w1 = wring[:, r * 1024:r * 1024 + 512]
                pe.wait_ge(s["xt"], e + 1)
                for n in range(NB):
                    pe.matmul(bank[2 + n][:, 0:CAP], w1[:, n * P:(n + 1) * P], qx[:, r % 2, 0:CAP],
                              start=True, stop=True).then_inc(s["hm"], 1)

            def down(e, r):
                w2 = wring[:, r * 1024 + 512:r * 1024 + 1024]
                pe.wait_ge(s["ye"], e + 1)
                for t in range(ST):
                    for n in range(NB):
                        if t == 0:
                            pe.wait_ge(s["hr" if n % 2 == 0 else "hh2"], 2 * e + n // 2 + 1)
                        last = pe.matmul(bank[6 + r % 2][:, t * P:(t + 1) * P], hid[:, r % 2, n, t * P:(t + 1) * P],
                                         w2[:, n * D:(n + 1) * D], start=(n == 0), stop=(n == NB - 1))
                last.then_inc(s["ym"], 1)

            pe.wait_ge(s["xl0"], 16)
            turn(0, 0)

            def expert(e, g, r, more=True):
                pe.wait_ge(s[f"w{r}"], 32 * (g + 1))
                hidden(e, r)
                if more:
                    pe.wait_ge(s[f"xl{(r + 1) % 2}"], 8 * (e + 1 - (r + 1) % 2) + 16)
                    turn(e + 1, (r + 1) % 2)
                down(e, r)

            with pe.Fori(0, E // 4 - 1) as g:
                for r in range(4):
                    expert(4 * g + r, g, r)
            for r in range(4):
                expert(E - 4 + r, E // 4 - 1, r, r < 3)

        @block.vector
        def _(dve):
            link = Chain(dve, s["dch"])
            dve.memset(zeros, 0.0).then_inc(s["zero"], 1)
            dve.memset(ones16[:, :], 1.0).then_inc(s["zero"], 1)
            link(dve.memset(reset[:, :, :], 1.0))
            link(dve.memset(reset[:, :, 0:1], 0.0))
            dve.wait_ge(s["consts"], 16)
            dve.tensor_copy(upper16[:, :], upper).then_inc(s["zero"], 1)
            dve.wait_ge(s["t_small"], 1)
            dve.tensor_copy(smallT[:, :], bank[0][:, 0:80]).then_inc(s["smallT"], 1)
            dve.wait_ge(s["e_silu"], 1)
            link(dve.tensor_scalar(silu[:, 1, :], silu[:, 0, :], 1.0, None, ALU.add))
            link(dve.reciprocal(silu[:, 2, :], silu[:, 1, :]))
            dve.tensor_tensor(silu[:, 3, :], silu[:, 2, :], smallT[:, 8:16], ALU.mult).then_inc(s["silu"], 1)
            dve.wait_ge(s["silu"], 1)
            sbc = prob[:, 1, :, :].rearrange("p a w -> p (a w)")[:, 0:B * P].rearrange("p (b w) -> p b w", b=B)
            dve.tensor_copy(sbc, silu[:, 3, :, None].to_broadcast([P, B, P])).then_inc(s["silu"], 1)
            dve.wait_ge(s["t_pos"], 1)
            for i in range(2):
                dve.tensor_copy(posT[:, :, i, :], bank[1][:, 0:PAIRS * FREQS].rearrange("p (a f) -> p a f", f=FREQS))\
                    .then_inc(s["posT"], 1)
            wqT = prob[:, 0, :, :].rearrange("p a w -> p (a w)")
            for i in range(2):
                dve.wait_ge(s["t_wq"], i + 1)
                dve.tensor_copy(wqT[:, i * 512:(i + 1) * 512], bank[2 + i][:, :]).then_inc(s["wqT"], 1)

            def moments():
                me, mo, ve, vo = (stats[:, :, i] for i in (1, 4, 2, 5))
                link(dve.tensor_tensor(mom[:, 0, :], me, mo, ALU.add))
                link(dve.tensor_tensor(mom[:, 1, :], me, mo, ALU.subtract))
                link(dve.tensor_tensor(mom[:, 2, :], ve, vo, ALU.add))
                link(dve.tensor_tensor(mom[:, 3, :], mom[:, 1, :], mom[:, 1, :], ALU.mult))
                link(dve.scalar_tensor_tensor(mom[:, 1, :], mom[:, 3, :], D / 4.0, mom[:, 2, :], ALU.mult, ALU.add))
                link(dve.tensor_scalar(mom[:, 0, :], mom[:, 0, :], 0.5, None, ALU.mult))
                dve.tensor_scalar(mom[:, 4, :], mom[:, 1, :], 1.0 / D, EPS, ALU.mult, ALU.add).then_inc(s["rst"], 1)

            for i in range(2):
                dve.wait_ge(s[f"x{i}"], 16)
                with dve.Fori(0, TILES // 8) as t:
                    for q in range(4):
                        n = 16 * i + 4 * t + q
                        last = dve.bn_stats(stats[:, bass.ds(n, 1), :].rearrange("p a s -> p (a s)"),
                                            x[:, bass.ds(n, 1), :].rearrange("p a d -> p (a d)"))
                    last.then_inc(s["mm0"], 1)
            dve.wait_ge(s["mm0"], 2 * (TILES // 8))
            moments()
            dve.wait_ge(s["mod_mm"], 1)
            dve.tensor_copy(modT[:, 0, :], bank[0][:, 0:B]).then_inc(s["modT"], 1)
            dve.tensor_scalar(modT[:, 1, :], bank[0][:, B:2 * B], 1.0, None, ALU.add).then_inc(s["modT"], 1)
            for b in range(B):
                dve.wait_ge(s["bc_mm"], b + 1)
                dve.tensor_copy(modb[:, b, :, :], bank[2 + b % 2][:, :].rearrange("p (a d) -> p a d", a=4))\
                    .then_inc(s["modb"], 1)
            dve.wait_ge(s["rs1"], 1)
            with dve.Fori(0, B // 2) as t:
                for r in range(2):
                    b = 2 * t + r
                    if r == 0:
                        dve.wait_ge(s["t_x"], b)
                    for q in range(QT):
                        n = b * QT + q
                        last = dve.tensor_scalar(xn[:, r, q, :], x[:, bass.ds(n, 1), :].rearrange("p a d -> p (a d)"),
                                                 mom[:, 0, bass.ds(n, 1)], mom[:, 5, bass.ds(n, 1)],
                                                 ALU.subtract, ALU.mult)
                    last.then_inc(s["xn1"], 1)

            def scores(j, par, k):
                q = ORDER[k % QT]
                w = P * (q + 1)
                waits(dve, ("consts", 16), ("sc", 8 * j + k + 1), ("ex", 8 * j + k - 3))
                dve.tensor_tensor_reduce(out=srow[:, k % 4, 0:w], in0=scb[k % 2][:, 0:w], in1=mask[:, S - w:S],
                                         scale=-1.0, scalar=BIG, op0=ALU.add, op1=ALU.min,
                                         accum_out=nmax[:, par, k:k + 1]).then_inc(s["tt"], 1)

            def evac_pt(j, g):
                dve.wait_ge(s["tr"], 6 * j + g + 1)
                dve.tensor_copy(pt[:, 0, KOFF[g]:KOFF[g] + GW[g]], trb[g % 2][:, 0:GW[g]]).then_inc(s["evA"], 1)

            def recip(j, par, h):
                dve.wait_ge(s["ex"], 8 * j + 4 * h + 4)
                dve.reciprocal(rsum[:, par, 4 * h:4 * h + 4], sums[:, par, 4 * h:4 * h + 4]).then_inc(s["rc"], 1)

            def evac_q(j, par, h):
                dve.wait_ge(s["qp"], 2 * j + h + 1)
                dve.scalar_tensor_tensor(qx[:, h, :], prb[h][:, :], wq[:, par, 3 * P + h:3 * P + h + 1], qtab,
                                         ALU.add, ALU.mult).then_inc(s["qe"], 1)

            def accumulate(j):
                dve.wait_ge(s["op"], j + 1)
                wait(dve, "ac", j)
                rows = acc[:, bass.ds(((j >> 3) & 7) * QT, QT), :]
                dve.tensor_tensor(rows, opb[:, :].rearrange("p (t d) -> p t d", t=QT), rows, ALU.add)\
                    .then_inc(s["ac"], 1)

            def step(j, par, before=True, after=True):
                for k in range(8):
                    scores(j, par, k)
                    if before and k < 3:
                        evac_pt(j - 1, k)
                    if k == 4:
                        recip(j, par, 0)
                        if after:
                            evac_q(j + 1, 1 - par, 0)
                recip(j, par, 1)
                if after:
                    evac_q(j + 1, 1 - par, 1)
                if before:
                    accumulate(j - 1)

            dve.wait_ge(s["accz"], 1)
            dve.wait_ge(s["wall"], 7)
            dve.wait_ge(s["wld0"], 16)
            evac_q(0, 0, 0)
            evac_q(0, 0, 1)
            step(0, 0, before=False)
            with dve.Fori(0, NJ // 2 - 1) as t:
                step(2 * t + 1, 1)
                step(2 * t + 2, 0)
            step(NJ - 1, 1, after=False)
            for g in range(3):
                evac_pt(NJ - 1, g)
            accumulate(NJ - 1)

            link(dve.tensor_scalar(modb[:, :, 2, :], modb[:, :, 2, :], 1.0, None, ALU.add))
            tmp = [qx[:, :, :].rearrange("p a (b d) -> p (a b) d", d=D), kx[:, :, :].rearrange("p a (b d) -> p (a b) d", d=D)]
            dve.wait_ge(s["ac"], NJ)
            for i in (0, 3):
                g_ = modb[:, :, i, :]
                link(dve.tensor_scalar(tmp[1], g_, 0.0, 2.0, ALU.is_ge, ALU.mult))
                link(dve.scalar_tensor_tensor(tmp[0], tmp[1], -1.0, g_, ALU.add, ALU.mult))
                link(dve.tensor_scalar(tmp[0], tmp[0], 0.25, None, ALU.max))
                link(dve.scalar_tensor_tensor(g_, tmp[1], -1.0, tmp[0], ALU.add, ALU.mult))
            with dve.Fori(0, B) as b:
                rows, xr = acc[:, bass.ds(b * QT, QT), :], x[:, bass.ds(b * QT, QT), :]
                dve.tensor_tensor(rows, rows, modb[:, bass.ds(b, 1), 0, :].to_broadcast([P, QT, D]), ALU.mult)\
                    .then_inc(s["ac"], 1)
                dve.wait_ge(s["ac"], b + NJ + 1)
                dve.tensor_tensor(xr, xr, rows, ALU.add).then_inc(s["x2"], 1)
                dve.wait_ge(s["x2"], b + 1)
                for q in range(QT):
                    n = b * QT + q
                    last = dve.bn_stats(stats[:, bass.ds(n, 1), :].rearrange("p a s -> p (a s)"),
                                        x[:, bass.ds(n, 1), :].rearrange("p a d -> p (a d)"))
                last.then_inc(s["mm0"], 1)
            dve.wait_ge(s["mm0"], 2 * (TILES // 8) + B)
            moments()
            dve.wait_ge(s["rs2"], 1)
            dve.scalar_tensor_tensor(mom[:, 0, :], mom[:, 0, :], -1.0, mom[:, 5, :], ALU.mult, ALU.mult)\
                .then_inc(s["x2"], 1)
            with dve.Fori(0, B) as b:
                dve.wait_ge(s["xh"], b + 1)
                rows = acc[:, bass.ds(b * QT, QT), :]
                dve.tensor_tensor(rows, rows, modb[:, bass.ds(b, 1), 2, :].to_broadcast([P, QT, D]), ALU.mult)\
                    .then_inc(s["h2a"], 1)
            with dve.Fori(0, B // 2) as t:
                for r in range(2):
                    b = 2 * t + r
                    dve.wait_ge(s["h2"], b + 1)
                    if r == 0:
                        dve.wait_ge(s["t_h"], b)
                    dve.tensor_copy(hst[:, r, :, :], acc[:, bass.ds(b * QT, QT), :]).then_inc(s["h2a"], 1)
                    dve.wait_ge(s["lg"], b + 1)
                    dve.tensor_tensor(lgt.rearrange("p (t e) -> p t e", e=E)[:, bass.ds(b * QT, QT), :],
                                      bank[2][:, 0:QT * E].rearrange("p (t e) -> p t e", e=E),
                                      bg[:, None, :].to_broadcast([P, QT, E]), ALU.add).then_inc(s["lge"], 1)
            dve.wait_ge(s["lge"], B)
            te = lambda a: a.rearrange("p (t e) -> p t e", e=E)
            wide = lambda a: a[:, :, None].to_broadcast([P, TILES, E])
            lmax, esum, gate, emax, where, keep, tmp1, tmp2 = (rsm[:, i, :] for i in range(8))
            link(dve.tensor_reduce(lmax, te(lgt), AX.X, ALU.max))
            dve.tensor_tensor(te(rt[0]), te(lgt), wide(lmax), ALU.subtract).then_inc(s["lge"], 1)
            dve.wait_ge(s["lge"], B + 1)
            link(dve.scalar_tensor_tensor(te(rt[2]), te(rt[0]), 0.0, desc[:, None, :].to_broadcast([P, TILES, E]),
                                          ALU.is_ge, ALU.mult))
            link(dve.tensor_reduce(emax, te(rt[2]), AX.X, ALU.max))
            dve.tensor_tensor(te(oh16[:, :]), te(rt[2]), wide(emax), ALU.is_equal).then_inc(s["oh"], 1)
            dve.wait_ge(s["lge"], B + 2)
            link(dve.tensor_reduce(esum, te(rt[1]), AX.X, ALU.add))
            link(dve.reciprocal(gate, esum))
            dve.wait_ge(s["pre"], 1)
            et = lambda a: a.rearrange("p (e t) -> p e t", e=E)
            link(dve.tensor_copy(et(rt[0]), bank[4][:, :].rearrange("p (t e) -> p e t", e=E)))
            link(dve.tensor_tensor_scan(rt[1], reset[:, :, :].rearrange("p e t -> p (e t)"), rt[0], 0.0, ALU.mult, ALU.add))
            link(dve.tensor_tensor(rt[2], rt[1], rt[0], ALU.subtract))
            link(dve.tensor_tensor(te(rt[3]), te(bank[3][:, :]), rt[2].rearrange("p (e t) -> p t e", e=E), ALU.add))
            link(dve.tensor_tensor(rt[0], rt[3], oh16[:, :], ALU.mult))
            link(dve.tensor_reduce(where, te(rt[0]), AX.X, ALU.add))
            link(dve.tensor_scalar(keep, where, float(CAP), None, ALU.is_lt))
            link(dve.tensor_tensor(gate, gate, keep, ALU.mult))
            link(dve.tensor_scalar(tmp1, where, float(CAP - 1), float(E * CAP), ALU.min, ALU.add))
            link(dve.scalar_tensor_tensor(tmp2, emax, -float(CAP), tmp1, ALU.mult, ALU.add))
            link(dve.tensor_copy(gidx[:, :], tmp2))
            link(dve.tensor_scalar(tmp1, keep, -2.0 * E * CAP, 2.0 * E * CAP, ALU.mult, ALU.add))
            link(dve.tensor_tensor(sidx[:, :], tmp2, tmp1, ALU.add))

            dve.memset(rsm[:, 8, :], 0.0).then_inc(s["ye"], 2)
            dve.memset(rsm[:, 9, :], 0.0).then_inc(s["idx"], 1)

            def expert(e, par):
                for n in range(1, NB, 2):
                    dve.wait_ge(s["hm"], NB * e + n + 1)
                    dve.tensor_scalar(hid[:, par, n, :], bank[2 + n][:, 0:CAP], smallT[:, bass.ds(16 + NB * e + n, 1)],
                                      0.0, ALU.add, ALU.max).then_inc(s["hh2"], 1)
                dve.wait_ge(s["ym"], e + 1)
                wait(dve, f"ys{par}", 8 * (e - par))
                dve.tensor_tensor(xn[:, par, 2:4, :], bank[6 + par][:, 0:CAP].rearrange("p (t d) -> p t d", t=ST),
                                  b2[:, bass.ds(e, 1), :].to_broadcast([P, ST, D]), ALU.add).then_inc(s["ye"], 1)

            dve.wait_ge(s["scat"], 16 * TILES)
            expert(0, 0)
            expert(1, 1)
            with dve.Fori(1, E // 2) as g:
                expert(2 * g, 0)
                expert(2 * g + 1, 1)
            yg = hT[:, :].rearrange("p (t d) -> p t d", d=D)
            for b in range(B):
                dve.wait_ge(s[f"gat{b}"], 16 * QT)
                for q in range(QT):
                    t = b * QT + q
                    last = dve.scalar_tensor_tensor(yg[:, t, :], yg[:, t, :], gate[:, t:t + 1], modb[:, b, 3, :],
                                                    ALU.mult, ALU.mult)
                link(last)
                rows = x[:, b * QT:(b + 1) * QT, :]
                dve.tensor_tensor(rows, rows, yg[:, b * QT:(b + 1) * QT, :], ALU.add).then_inc(s["fin"], 1)


def host_constants():
    k = np.arange(S, dtype=np.float64)
    f = np.arange(FREQS)
    inv = 1250.0 ** (-(f // 2 * 2) / FREQS)
    ang = inv[:, None] * k[None, :]
    even = (f % 2 == 0)[:, None]
    sig = np.sqrt(2.0) * FREQS ** -0.5
    cq = C_QKV * HD ** -0.5
    qtab = np.concatenate([np.full((HD, S), cq),
                           cq * sig * np.where(even, np.sin(ang), np.cos(ang)),
                           cq * sig * np.where(even, -np.cos(ang), np.sin(ang))])
    ktab = np.concatenate([np.cos(ang), np.sin(ang)])
    causal = np.where(np.arange(P)[None, :] > np.arange(P)[:, None], NEG, 0.0)
    mask = np.concatenate([np.zeros((P, S - P)), causal], axis=1)
    desc = np.broadcast_to(E - np.arange(E), (P, E))
    upper = (np.arange(P)[:, None] < np.arange(P)[None, :]).astype(np.float64)
    consts = np.concatenate([np.eye(P), mask, qtab, desc, upper], axis=1)
    return np.ascontiguousarray(consts, dtype=np.float32), np.ascontiguousarray(ktab, dtype=np.float32)


NAMES = ["L0_attn_input", "L0_attn_qkv", "L0_attn_q_bias", "L0_attn_positional", "L0_attn_out_kernel",
         "L0_attn_out_bias", "L0_ffn_Wg", "L0_ffn_bg", "L0_ffn_W1", "L0_ffn_b1", "L0_ffn_W2", "L0_ffn_b2",
         "L0_c", "L0_wmod"]


def kernel(**inputs):
    import concourse.bacc as bacc
    from concourse.bass_utils import run_bass_kernel_spmd

    nc = bacc.Bacc("TRN2", target_bir_lowering=False, num_devices=1)
    arrays, args = {}, []
    consts, ktab = host_constants()
    for name, a in [(n, np.ascontiguousarray(inputs[n])) for n in NAMES] + [("consts", consts), ("ktab", ktab)]:
        arrays[f"in_{name}"] = a
        args.append(nc.dram_tensor(f"in_{name}", a.shape, mybir.dt.from_np(a.dtype), kind="ExternalInput").ap())
    out = nc.dram_tensor("out_0", (B, S, D), F32, kind="ExternalOutput").ap()
    program(nc, *args, out)
    r = run_bass_kernel_spmd(nc, [arrays], core_ids=[0])
    return r.results[0]["out_0"]
```

```python
from contextlib import ExitStack

import numpy as np
import concourse.bass as bass
from concourse import mybir

F32 = mybir.dt.float32
F32R = mybir.dt.float32r
BF16 = mybir.dt.bfloat16
U32 = mybir.dt.uint32
ALU = mybir.AluOpType
ACT = mybir.ActivationFunctionType
AX = mybir.AxisListType

P = 128
B, S, D = 8, 512, 128
HEADS, HD, FREQS = 16, 64, 32
PAIRS = HEADS // 2
NJ = B * PAIRS
TILES = B * S // P
QT = S // P
E, FF = 16, 512
CAP = B * S // E
NB = FF // P
ST = CAP // P
EPS = 1e-5
C_QKV = (3.0 * D * HD * HEADS) ** -0.25
C_OUT = (HEADS * HD * D) ** -0.25
NEG = -1e30
BIG = 3e38
WP = 2 * P + P
RW = 3 * D + 1
NOWHERE = 8 * B * S
LINKS = 26
GW = [S, 384, 384]
GROUPS = [[(q, 0) for q in range(4)], [(q, 1) for q in range(1, 4)], [(2, 2), (3, 2), (3, 3)]]
QOFF = [0, 128, 384, 768]
KOFF = [0, 512, 896, 1152]
PW = 1280
V_OF = [(0, 0, 3)] + [(0, 1, t) for t in range(4)] + [(1, 0, t) for t in range(3)]
V_BANKS = [2, 3, 0]
TURN = [0, 1, 2, 3, 4, 5]
ORDER = [3, 2, 1, 0]


def program(nc, x_d, qkv_d, qb_d, pos_d, wo_d, bo_d, wg_d, bg_d, w1_d, b1_d, w2_d, b2_d, c_d, wmod_d,
            consts_d, ktab_d, out_d):
    ctx = ExitStack()
    with ctx:
        def sb(name, shape, dt=F32):
            return ctx.enter_context(nc.sbuf_tensor(name, shape, dt))

        def sem(name):
            return ctx.enter_context(nc.semaphore(name))

        x = sb("x", [P, TILES, D])
        acc = sb("acc", [P, QT, D])
        modb = sb("modb", [P, B, 4, D])
        whi = sb("whi", [P, PAIRS, WP], F32R)
        wlo = sb("wlo", [P, PAIRS, WP], F32R)
        wvhi = sb("wvhi", [P, HEADS * HD], F32R)
        wvlo = sb("wvlo", [P, HEADS * HD], F32R)
        raw = sb("raw", [P, 4 * HEADS * HD])
        qkv = raw[:, 0:3 * HEADS * HD].rearrange("p (i w) -> p i w", i=3)
        pos = raw[0:FREQS, 3 * HEADS * HD:]
        wo = sb("wo", [P, PAIRS, D])
        wmod = sb("wmod", [P, 6, D])
        consts = sb("consts", [P, 128 + 512 + 512 + 16 + 128 + TILES])
        ident = consts[:, 0:128]
        mask = consts[:, 128:640]
        qtab = consts[:, 640:1152]
        desc = consts[:, 1152:1168]
        upper = consts[:, 1168:1296]
        token = consts[:, 1296:1296 + TILES]
        small = sb("small", [80, P])
        smallT = sb("smallT", [P, 80])
        qbias = sb("qbias", [P, 2, PAIRS])
        posT = sb("posT", [P, PAIRS, 2, 2, FREQS])
        wg = sb("wg", [P, E])
        bg = sb("bg", [P, E])
        bo = sb("bo", [P, D])
        silu = sb("silu", [P, 4, B])
        mrow = sb("mrow", [B, 4, D])
        modT = sb("modT", [P, 4, B])
        stats = sb("stats", [P, 2, QT, 6])
        mom = sb("mom", [P, 2, 6, QT])
        mhalf = sb("mhalf", [P, QT])
        xn = sb("xn", [P, QT, D])
        hn = sb("hn", [P, S])
        vhi = sb("vhi", [P, S], F32R)
        vlo = sb("vlo", [P, S], F32R)
        hhi = sb("hhi", [P, 2, S], F32R)
        hlo = sb("hlo", [P, 2, S], F32R)
        row = sb("row", [P, QT, RW])
        fill = sb("fill", [P, RW])
        h2T = sb("h2T", [P, S])
        xh = sb("xh", [P, QT, D])
        mtmp = xh[0:B, :, :].rearrange("p (i g) d -> p i g d", i=2)
        lgt = sb("lgt", [P, 5, QT * E])
        oh16 = sb("oh16", [P, QT * E], BF16)
        rsm = sb("rsm", [P, 10, QT])
        base = sb("base", [P, E])
        sidx = sb("sidx", [P, QT], U32)
        upper16 = sb("upper16", [P, P], BF16)
        ones16 = sb("ones16", [P, P], BF16)
        qx = sb("qx", [P, 2, S])
        qhi = sb("qhi", [P, 2, S - P], F32R)
        qlo = sb("qlo", [P, 2, S - P], F32R)
        kx = sb("kx", [P, 2, P])
        khi = sb("khi", [P, 2, S], F32R)
        klo = sb("klo", [P, 2, S], F32R)
        v = sb("v", [P, 2, QT, S])
        srow = sb("srow", [P, 4, S])
        nmax = sb("nmax", [P, 2, 8])
        sums = sb("sums", [P, 2, 8])
        rsum = sb("rsum", [P, 2, 8])
        prob = sb("prob", [P, 2, 2, PW])
        pt = sb("pt", [P, 2, PW])
        oT = sb("oT", [P, S])
        early = raw[:, :].rearrange("p (r i n d) -> p r i n d", r=4, i=2, n=NB)
        wring = [early[:, r] for r in range(4)] + \
            [prob[:, :, :, :].rearrange("p a b w -> p (a b w)")[:, r * 1024:(r + 1) * 1024]
             .rearrange("p (i n d) -> p i n d", i=2, n=NB) for r in range(4)]
        b2 = v[:, 0, :, :].rearrange("p t s -> p (t s)").rearrange("p (e d) -> p e d", e=E)
        xf = x[:, :, :].rearrange("p t d -> p (t d)")
        slots = xf[:, 0:4 * ST * RW].rearrange("p (a t w) -> p a t w", a=4, t=ST)
        hid = srow[:, :, :].rearrange("p k s -> p (k s)").rearrange("p (a n c) -> p a n c", a=2, n=NB)
        ye = row[:, :, 0:D].rearrange("p (a t) d -> p a t d", a=2)
        yidx = sb("yidx", [P, 2, ST], U32)
        bank = [ctx.enter_context(nc.psum_tensor(f"bank{i}", [P, 512], F32)) for i in range(8)]
        scb, trb, prb, otb, opb = bank[0:2], bank[2:4], bank[4:6], bank[6], bank[7]
        xbuf = nc.dram_tensor("xbuf", [E * CAP, RW], F32).ap()
        mod_dram = nc.dram_tensor("mod_rows", [B, 4 * D], F32).ap()

        names = ("ident consts small pos w_q w_k w_v ktab x0 x1 wmod misc b2 wo zero "
                 "t_small smallT e_silu silu t_pos posT t_wq wqT wg_mm bias whi wlo wlo_k mod_mm modT mev mrow modb gates "
                 "st rst1 rs1 xn t_x hn vhi vlo hld wv qh ql kl kt "
                 "sc tt ex rc nm tr evA evB pv oe qp qe kp ke vp ve op ac "
                 "dch pch x2 rst2 rs2 xh h2a h2 t_h hh lg lge lm lex oh gate gg pre prx idx scat filled x2st "
                 "xl0 xl1 xl2 xl3 w0 w1 w2 w3 w4 w5 w6 w7 tx xt hm hr hh2 ym y yi ysc0 ysc1").split()
        s = {n: sem("s_" + n) for n in names}

        class Chain:

            def __init__(self, eng, semaphore):
                self.eng, self.sem, self.base, self.n = eng, semaphore, 0, 0

            def __call__(self, ins):
                self.n += 1
                ins.then_inc(self.sem, 1)
                self.eng.wait_ge(self.sem, self.base + self.n)

            def enter(self, turns, per):
                self.before, self.per = self.base + self.n, per
                self.base, self.n = self.before + per * turns, 0

            def leave(self, turns):
                assert self.n == self.per, self.n
                self.base, self.n = self.before + self.per * turns, 0

        def wait(eng, name, value):
            if not isinstance(value, int) or value > 0:
                eng.wait_ge(s[name], value)

        def waits(eng, *pairs):
            values = [v if isinstance(v, int) else eng.compute_val(v) for _, v in pairs]
            for (name, _), v in zip(pairs, values):
                wait(eng, name, v)

        def batches(eng, turn, enter=None, leave=None):
            turn(0, True, False)
            with eng.Fori(1, B - 1) as b:
                if enter:
                    enter(b - 1)
                turn(b, False, False)
            if leave:
                leave(B - 2)
            turn(B - 1, False, True)

        def g_of(tile, i):
            return tile[:, 4 * i:4 * i + 4, 0:2 * P].rearrange("p a (h c) -> p a h c", h=2)[:, :, :, HD:P]

        def one(tile, b, *rest):
            return tile[(slice(None), bass.ds(b, 1)) + rest]

        block = ctx.enter_context(nc.Block())

        @block.sync
        def _(sp):
            sp.dma_start(ident, consts_d[:, 0:128]).then_inc(s["ident"], 16)
            sp.dma_start(small[0:8, :], qb_d.rearrange("(a h) d -> a (h d)", h=2)).then_inc(s["small"], 16)
            sp.dma_start(small[8:16, :], c_d).then_inc(s["small"], 16)
            sp.dma_start(small[16:80, :], b1_d.rearrange("e (n p) -> (e n) p", p=P)).then_inc(s["small"], 16)
            xt_d = x_d.rearrange("b (t p) d -> p (b t) d", p=P)
            sp.dma_start(x[:, 0:QT, :], xt_d[:, 0:QT, :]).then_inc(s["x0"], 16)
            sp.dma_start(wmod[:, :, :], wmod_d.rearrange("p (a b) -> p a b", a=6)).then_inc(s["wmod"], 16)
            sp.dma_start(consts[:, 128:], consts_d[:, 128:]).then_inc(s["consts"], 16)
            for h in range(2):
                sp.dma_start(kx[HD:P, h, :], ktab_d[:, 0:P]).then_inc(s["ktab"], 16)
            sp.dma_start(h2T[HD:P, :], ktab_d).then_inc(s["ktab"], 16)
            sp.dma_start(bo[:, :], bo_d.rearrange("(a n) -> a n", a=1).to_broadcast([P, D])).then_inc(s["misc"], 16)
            sp.dma_start(wg[:, :], wg_d).then_inc(s["misc"], 16)
            sp.dma_start(bg[:, :], bg_d.rearrange("(a n) -> a n", a=1).to_broadcast([P, E])).then_inc(s["misc"], 16)
            sp.dma_start(x[:, QT:TILES, :], xt_d[:, QT:TILES, :]).then_inc(s["x1"], 16)
            sp.dma_start(wo[:, :, :], wo_d.rearrange("(a p) d -> p a d", p=P)).then_inc(s["wo"], 16)
            out_v = out_d.rearrange("b (t p) d -> p b t d", p=P)

            def weights(e, slot):
                sp.dma_start(wring[slot][:, 0, :, :], w1_d[e].rearrange("p (n d) -> p n d", n=NB))\
                    .then_inc(s[f"w{slot}"], 16)
                sp.dma_start(wring[slot][:, 1, :, :], w2_d[e].rearrange("(n p) d -> p n d", p=P))\
                    .then_inc(s[f"w{slot}"], 16)

            def rows(e, slot):
                sp.dma_start(slots[:, slot, :, :], xbuf.rearrange("(e t p) w -> e p t w", p=P, t=ST)[e])\
                    .then_inc(s[f"xl{slot}"], 16)

            def at(value):
                return value if isinstance(value, int) else sp.compute_val(value)

            def turn(b, first, last):
                if first:
                    sp.wait_ge(s["gates"], 1)
                    sp.dma_start(mod_dram, mrow[:, :, :].rearrange("p a d -> p (a d)")).then_inc(s["mrow"], 16)
                    sp.wait_ge(s["mrow"], 16)
                    sp.dma_start(modb[:, :, :, :].rearrange("p b a d -> p (b a d)"),
                                 mod_dram.rearrange("(o b) w -> o (b w)", o=1).to_broadcast([P, B * 4 * D]))\
                        .then_inc(s["modb"], 16)
                    sp.wait_ge(s["zero"], 2)
                    for q in range(4):
                        sp.dma_start(xbuf.rearrange("(p r) w -> p r w", p=P)[:, 8 * q:8 * q + 8, :],
                                     fill[:, None, :].to_broadcast([P, 8, RW])).then_inc(s["filled"], 16)
                    sp.wait_ge(s["wlo_k"], 1)
                    sp.wait_ge(s["wlo"], 4)
                    sp.wait_ge(s["wv"], 2)
                    sp.wait_ge(s["t_wq"], 2)
                    sp.wait_ge(s["t_pos"], 1)
                    for e in range(4):
                        weights(e, e)
                else:
                    store(b)

            def store(b):
                p = at(b - 1)
                sp.wait_ge(s["x2"], b)
                sp.dma_start(out_v[:, bass.ds(p, 1), :, :].rearrange("p a t d -> p (a t) d"),
                             row[:, :, D:2 * D]).then_inc(s["x2st"], 16)

            batches(sp, turn)
            store(B)
            sp.wait_ge(s["pv"], NJ)
            for e in range(4, 8):
                weights(e, e)
            sp.dma_start(b2, b2_d.rearrange("(a e) d -> a e d", a=1).to_broadcast([P, E, D])).then_inc(s["b2"], 16)
            sp.wait_ge(s["scat"], 64 * B)
            for e in range(4):
                rows(e, e)
            for e in range(E - 3):
                if e < E - 8:
                    sp.wait_ge(s["ym"], e + 1)
                    weights(e + 8, e)
                sp.wait_ge(s["y"], e + 1)
                rows((e + 4) % E, e % 4)

        @block.gpsimd
        def _(gp):
            def rstd(i, n):
                waits(gp, ("pch", 1), (f"rst{i + 1}", n))
                gp.tensor_tensor(mom[:, i, 5, :], mom[:, i, 4, :], mhalf[:, :], ALU.pow).then_inc(s[f"rs{i + 1}"], 1)

            gp.memset(posT[:, :, :, :, :], 0.0).then_inc(s["posT"], 1)
            gp.memset(mhalf[:, :], -0.5).then_inc(s["pch"], 1)
            gp.wait_ge(s["pch"], 1)
            rstd(0, 1)
            gp.wait_ge(s["w_k"], 16)
            gp.wait_ge(s["whi"], 3)
            gp.tensor_tensor(wlo[:, :, 2 * P:3 * P], qkv[:, 1, :].rearrange("p (a w) -> p a w", a=PAIRS),
                             whi[:, :, 2 * P:3 * P], ALU.subtract).then_inc(s["wlo_k"], 1)
            gp.wait_ge(s["wlo_k"], 1)
            gp.wait_ge(s["kt"], 2)
            for h in range(2):
                gp.tensor_tensor(klo[HD:P, h, :], h2T[HD:P, :], khi[HD:P, h, :], ALU.subtract).then_inc(s["kt"], 1)
            gp.wait_ge(s["kt"], 4)

            def copy(n, i):
                half = gp.compute_val(n & 1) if not isinstance(n, int) else n & 1
                waits(gp, ("pch", 1), ("vhi", n + 1), ("vlo", n + 1))
                there, here = ((hhi, vhi), (hlo, vlo))[i]
                gp.tensor_copy(there[:, bass.ds(half, 1), :].rearrange("p a s -> p (a s)"), here[:, :])\
                    .then_inc(s["hld"], 1)

            def modulate(b):
                p = gp.compute_val(b - 1) if not isinstance(b, int) else b - 1
                waits(gp, ("modb", 16), ("xh", b))
                gp.tensor_tensor(row[:, :, 0:D], xh[:, :, :], one(modb, p, 2).to_broadcast([P, QT, D]), ALU.mult)\
                    .then_inc(s["h2a"], 1)
                gp.wait_ge(s["h2a"], b)
                gp.tensor_tensor(row[:, :, 0:D], row[:, :, 0:D], one(modb, p, 1).to_broadcast([P, QT, D]), ALU.add)\
                    .then_inc(s["h2"], 1)

            def gated(b):
                p = gp.compute_val(b - 1) if not isinstance(b, int) else b - 1
                waits(gp, ("modb", 16), ("gate", b))
                gp.tensor_tensor(row[:, :, 2 * D:3 * D], rsm[:, 2, :, None].to_broadcast([P, QT, D]),
                                 one(modb, p, 3).to_broadcast([P, QT, D]), ALU.mult).then_inc(s["gg"], 1)

            def scatter(b):
                waits(gp, ("filled", 64), ("gg", b), ("h2", b), ("idx", b), ("x2st", 16 * b))
                for t in range(QT):
                    gp.indirect_dma_start(out=xbuf, out_offset=bass.IndirectOffsetOnAxis(ap=sidx[:, t:t + 1], axis=0),
                                          in_=row[:, t, :], in_offset=None,
                                          bounds_check=E * CAP - 1, oob_is_err=False).then_inc(s["scat"], 16)

            def low_q(j, h):
                waits(gp, ("pch", 1), ("qh", 2 * j + h + 1))
                gp.tensor_tensor(qlo[:, h, :], qx[:, h, P:S], qhi[:, h, :], ALU.subtract).then_inc(s["ql"], 1)

            def divide(j, par, h, *others):
                waits(gp, ("pch", 1), ("rc", 2 * j + h + 1), *others)
                for q in range(QT):
                    part = prob[:, par, h, QOFF[q]:QOFF[q] + P * (q + 1)]
                    end = gp.tensor_scalar(part, part, rsum[:, par, 4 * h + q:4 * h + q + 1], 1.0,
                                           ALU.mult, ALU.mult)
                end.then_inc(s["nm"], 1)

            def turn(b, first, last):
                for a in range(PAIRS):
                    j = 8 * b + a
                    low_q(j, 1)
                    if not last:
                        if a == 1:
                            rstd(0, b + 2)
                        if a in (5, 6):
                            copy(b + 1, a - 5)
                    if not first:
                        if a == 2:
                            rstd(1, b)
                        if a == 3:
                            modulate(b)
                        if a == 6:
                            gated(b)
                        if a == 7:
                            scatter(b)
                    divide(j, a % 2, 0)
                    if not (last and a == PAIRS - 1):
                        low_q(j + 1, 0)
                    divide(j, a % 2, 1, *([("scat", 64 * b)] if a == 7 and not first else []))

            low_q(0, 0)
            batches(gp, turn)
            rstd(1, B)
            modulate(B)
            gated(B)
            scatter(B)

            def expert(e, par):
                waits(gp, ("pch", 1), ("y", e + 1), ("yi", e + 1))
                for t in range(ST):
                    gp.indirect_dma_start(out=out_d.rearrange("b s d -> (b s) d"),
                                          out_offset=bass.IndirectOffsetOnAxis(ap=yidx[:, par, t:t + 1], axis=0),
                                          in_=ye[:, par, t, :], in_offset=None,
                                          bounds_check=B * S - 1, oob_is_err=False).then_inc(s[f"ysc{par}"], 16)

            with gp.Fori(0, E // 2) as g:
                expert(2 * g, 0)
                expert(2 * g + 1, 1)
            for par in range(2):
                gp.wait_ge(s[f"ysc{par}"], 16 * ST * E // 2)

        @block.scalar
        def _(act):
            act.dma_start(pos[:, :], pos_d.rearrange("f n d -> f (n d)")).then_inc(s["pos"], 16)
            for i in range(3):
                act.dma_start(qkv[:, i, :], qkv_d.rearrange("p a n d -> p a (n d)")[:, i, :]).then_inc(s[f"w_{'qkv'[i]}"], 16)
            act.wait_ge(s["smallT"], 1)
            act.activation(silu[:, 0, :], smallT[:, 8:16], ACT.Exp, scale=-1.0).then_inc(s["e_silu"], 1)
            act.wait_ge(s["w_q"], 16)
            for h in range(2):
                act.activation(whi[:, :, h * P:h * P + HD],
                               qkv[:, 0, :].rearrange("p (a h d) -> p a h d", h=2, d=HD)[:, :, h, :], ACT.Copy)\
                    .then_inc(s["whi"], 1)
            act.wait_ge(s["w_k"], 16)
            act.activation(whi[:, :, 2 * P:3 * P], qkv[:, 1, :].rearrange("p (a w) -> p a w", a=PAIRS), ACT.Copy)\
                .then_inc(s["whi"], 1)
            act.wait_ge(s["w_v"], 16)
            act.activation(wvhi[:, :], qkv[:, 2, :], ACT.Copy).then_inc(s["wv"], 1)
            act.wait_ge(s["ktab"], 48)
            for h in range(2):
                act.activation(khi[HD:P, h, :], h2T[HD:P, :], ACT.Copy).then_inc(s["kt"], 1)
            for i in range(2):
                act.wait_ge(s["wg_mm"], i + 1)
                act.activation(g_of(whi, i), bank[4 + i][:, :].rearrange("p (a h w) -> p a h w", h=2, w=HD), ACT.Copy)\
                    .then_inc(s["whi"], 1)
            act.wait_ge(s["wg_mm"], 3)
            for h in range(2):
                act.activation(qbias[HD:P, h, :], bank[1][HD:P, 480 + h * PAIRS:480 + (h + 1) * PAIRS], ACT.Copy,
                               scale=1.0 / C_QKV).then_inc(s["bias"], 1)
                act.activation(qbias[0:HD, h, :], smallT[h * HD:(h + 1) * HD, 0:PAIRS], ACT.Copy,
                               scale=1.0 / C_QKV).then_inc(s["bias"], 1)

            def normed(n):
                act.wait_ge(s["t_x"], n + 1)
                wait(act, "vlo", n)
                act.activation(hn[:, :], opb[:, :], ACT.Identity, bias=modT[:, 0, bass.ds(n, 1)],
                               scale=modT[:, 1, bass.ds(n, 1)]).then_inc(s["hn"], 1)

            def high(n):
                act.wait_ge(s["hn"], n + 1)
                wait(act, "vp", 8 * n)
                wait(act, "hld", 2 * n)
                act.activation(vhi[:, :], hn[:, :], ACT.Copy).then_inc(s["vhi"], 1)

            def evac_k(j, h):
                act.wait_ge(s["kp"], j + 1)
                act.activation(khi[0:HD, h, :], prb[0][h * HD:(h + 1) * HD, :], ACT.Copy, scale=C_QKV)
                act.activation(kx[0:HD, h, :], prb[0][h * HD:(h + 1) * HD, 0:P], ACT.Copy, scale=C_QKV)\
                    .then_inc(s["ke"], 1)

            def high_q(j, h):
                act.wait_ge(s["qe"], 2 * j + h + 1)
                act.activation(qhi[:, h, :], qx[:, h, P:S], ACT.Copy).then_inc(s["qh"], 1)

            def evac_v(j, a):
                act.wait_ge(s["vp"], j + 4)
                n, g, t = V_OF[a]
                act.activation(v[:, g, t, :], prb[1][:, :], ACT.Copy).then_inc(s["ve"], 1)

            def exps(j, par, k):
                h, q = k // QT, ORDER[k % QT]
                act.wait_ge(s["tt"], 8 * j + k + 1)
                act.activation(prob[:, par, h, QOFF[q]:QOFF[q] + P * (q + 1)], srow[:, k % 4, 0:P * (q + 1)],
                               ACT.Exp, bias=nmax[:, par, k:k + 1], scale=-1.0,
                               accum_out=sums[:, par, 4 * h + q:4 * h + q + 1]).then_inc(s["ex"], 1)

            def evac_pt(j, i):
                act.wait_ge(s["tr"], 6 * j + i + 1)
                h, g = divmod(i, 3)
                act.activation(pt[:, h, KOFF[g]:KOFF[g] + GW[g]], trb[i % 2][:, 0:GW[g]], ACT.Copy)\
                    .then_inc(s["evB"], 1)

            def evac_o(j):
                act.wait_ge(s["pv"], j + 1)
                act.activation(oT[:, :], otb[:, :], ACT.Copy, scale=C_QKV * C_OUT).then_inc(s["oe"], 1)

            def second(b):
                act.wait_ge(s["t_h"], b)
                act.activation(h2T[:, :], opb[:, :], ACT.Identity, bias=modT[:, 2, bass.ds(b - 1, 1)],
                               scale=modT[:, 3, bass.ds(b - 1, 1)]).then_inc(s["hh"], 1)

            def gates(b):
                act.wait_ge(s["lm"], b)
                act.activation(lgt[:, 2, :], lgt[:, 1, :], ACT.Exp).then_inc(s["lex"], 1)

            def turn(b, first, last):
                for a in range(PAIRS):
                    step(8 * b + a, a % 2, b, a, first, last)

            def step(j, par, b, a, first, last):
                before, after = not (first and a == 0), not (last and a == PAIRS - 1)
                high_q(j, 1)
                for k in range(8):
                    if before and k == 5:
                        evac_pt(j - 1, 5)
                    exps(j, par, k)
                    if k == 1 and not (last and V_OF[a][0]):
                        evac_v(j, a)
                    if before and 2 <= k < 5:
                        evac_pt(j - 1, k)
                    if k == 4:
                        if a == 3 and not last:
                            normed(b + 1)
                        if a == 4 and not first:
                            second(b)
                    if k == 2 and a == 4 and not last:
                        high(b + 1)
                    if after and k == 5:
                        high_q(j + 1, 0)
                        evac_k(j + 1, 0)
                    if k == 6 and a == 5 and not first:
                        gates(b)
                if after:
                    evac_k(j + 1, 1)
                if before:
                    evac_o(j - 1)

            act.wait_ge(s["modT"], 2)
            normed(0)
            high(0)
            act.wait_ge(s["vhi"], 1)
            act.activation(hhi[:, 0, :], vhi[:, :], ACT.Copy).then_inc(s["hld"], 1)
            high_q(0, 0)
            for h in range(2):
                evac_k(0, h)
            for t in range(3):
                act.wait_ge(s["vp"], t + 1)
                act.activation(v[:, 0, t, :], bank[V_BANKS[t]][:, :], ACT.Copy).then_inc(s["ve"], 1)
            batches(act, turn)
            for i in range(2, 6):
                evac_pt(NJ - 1, i)
            evac_o(NJ - 1)
            second(B)
            gates(B)

            def expert(e, par):
                act.wait_ge(s["tx"], e + 1)
                act.activation(qx[:, par, 0:CAP], bank[par][:, 0:CAP], ACT.Copy).then_inc(s["xt"], 1)
                for n in range(0, NB, 2):
                    act.wait_ge(s["hm"], NB * e + n + 1)
                    act.activation(hid[:, par, n, :], bank[2 + n][:, 0:CAP], ACT.Relu,
                                   bias=smallT[:, bass.ds(16 + NB * e + n, 1)]).then_inc(s["hr"], 1)

            with act.Fori(0, E // 2) as g:
                expert(2 * g, 0)
                expert(2 * g + 1, 1)

        @block.tensor
        def _(pe):
            pe.wait_ge(s["ident"], 16)
            pe.wait_ge(s["small"], 48)
            pe.transpose(bank[0][:, 0:80], small[:, :], ident[0:80, 0:80]).then_inc(s["t_small"], 1)
            pe.wait_ge(s["pos"], 16)
            for a in range(PAIRS):
                last = pe.transpose(bank[1][:, a * FREQS:(a + 1) * FREQS], pos[:, a * P:(a + 1) * P],
                                    ident[0:FREQS, 0:FREQS])
            last.then_inc(s["t_pos"], 1)
            pe.wait_ge(s["w_q"], 16)
            for a in range(PAIRS):
                last = pe.transpose(bank[2 + a // 4][:, (a % 4) * P:(a % 4 + 1) * P], qkv[:, 0, a * P:(a + 1) * P],
                                    ident)
                if a % 4 == 3:
                    last.then_inc(s["t_wq"], 1)
            wqT = prob[:, 0, :, :].rearrange("p a w -> p (a w)")[:, 0:PAIRS * P]
            pe.wait_ge(s["posT"], 3)
            for a in range(PAIRS):
                pe.wait_ge(s["wqT"], 1 + a // 4)
                last = pe.matmul(bank[4 + a // 4][:, (a % 4) * P:(a % 4 + 1) * P], wqT[:, a * P:(a + 1) * P],
                                 posT[:, a, :, :, :].rearrange("p h i f -> p (h i f)"), start=True, stop=True)
                if a % 4 == 3:
                    last.then_inc(s["wg_mm"], 1)
            pe.wait_ge(s["silu"], 1)
            pe.wait_ge(s["wmod"], 16)
            for i, m in enumerate((0, 3, 1, 4)):
                pe.matmul(bank[0][:, i * B:(i + 1) * B], wmod[:, m, :], silu[:, 3, :], start=True, stop=True)
            pe.matmul(bank[6][0:B, :], silu[:, 3, :], wmod[:, 2:6, :].rearrange("p a d -> p (a d)"),
                      start=True, stop=True).then_inc(s["mod_mm"], 1)
            pe.wait_ge(s["smallT"], 1)
            for h in range(2):
                for a in range(PAIRS):
                    last = pe.matmul(bank[1][HD:P, 480 + h * PAIRS + a:481 + h * PAIRS + a],
                                     posT[:, a, h, :, :].rearrange("p i f -> p (i f)"),
                                     smallT[:, a:a + 1], start=True, stop=True)
            last.then_inc(s["wg_mm"], 1)

            def turn_x(n):
                pe.wait_ge(s["xn"], n + 1)
                for q in range(QT):
                    last = pe.transpose(opb[:, q * P:(q + 1) * P], xn[:, q, :], ident)
                last.then_inc(s["t_x"], 1)

            turn_x(0)

            def project(out, a, cols, n, name):
                if n is None:
                    hi, lo = vhi[:, :], vlo[:, :]
                else:
                    hi, lo = (t[:, bass.ds(n & 1, 1), :].rearrange("p a s -> p (a s)") for t in (hhi, hlo))
                for i, (w, h) in enumerate(((whi, hi), (whi, lo), (wlo, hi))):
                    last = pe.matmul(out, w[:, a, cols], h, start=(i == 0), stop=(i == 2))
                last.then_inc(s[name], 1)

            def project_q(j, n, a, h, ve=0):
                if n is None:
                    pe.wait_ge(s["vlo"], 1)
                elif h == 0:
                    pe.wait_ge(s["hld"], 2 * (n + 1))
                else:
                    wait(pe, "ve", ve)
                project(prb[h][:, :], a, slice(h * P, (h + 1) * P), n, "qp")

            def project_k(j, n, a):
                pe.wait_ge(s["qe"], 2 * j + 1)
                project(prb[0][:, :], a, slice(2 * P, 3 * P), n, "kp")

            def project_v(out, g, t):
                cols, rows = slice(g * S, (g + 1) * S), slice(t * P, (t + 1) * P)
                for i, (h, w) in enumerate(((vhi, wvhi), (vhi, wvlo), (vlo, wvhi))):
                    last = pe.matmul(out[:, :], h[:, rows], w[:, cols], start=(i == 0), stop=(i == 2))
                last.then_inc(s["vp"], 1)

            def scores(j, k):
                h, q = k // QT, ORDER[k % QT]
                if k % QT == 0:
                    pe.wait_ge(s["ql"], 2 * j + h + 1)
                    pe.wait_ge(s["kl"], 2 * j + h + 1)
                wait(pe, "tt", 8 * j + k - 1)
                out = scb[k % 2][:, 0:P * (q + 1)]
                if q == 0:
                    last = pe.matmul(out, qx[:, h, 0:P], kx[:, h, :], start=True, stop=True)
                else:
                    for i, (a, b) in enumerate(((qhi, khi), (qhi, klo), (qlo, khi))):
                        last = pe.matmul(out, a[:, h, (q - 1) * P:q * P], b[:, h, 0:P * (q + 1)],
                                         start=(i == 0), stop=(i == 2))
                last.then_inc(s["sc"], 1)

            def transposes(j, par, h, g):
                if g == 0:
                    pe.wait_ge(s["nm"], 2 * j + h + 1)
                i = 3 * h + g
                if i >= 2:
                    n = i - 2
                    pe.wait_ge(s["evA" if n < 2 else "evB"], 2 * j + n + 1 if n < 2 else 4 * j + n - 1)
                for n, (q, k) in enumerate(GROUPS[g]):
                    last = pe.transpose(trb[i % 2][:, n * P:(n + 1) * P],
                                        prob[:, par, h, QOFF[q] + k * P:QOFF[q] + (k + 1) * P], ident)
                last.then_inc(s["tr"], 1)

            def weighted(j, a, ve):
                pe.wait_ge(s["evA"], 2 * j + 2)
                pe.wait_ge(s["evB"], 4 * j + 4)
                pe.wait_ge(s["ve"], ve)
                wait(pe, "oe", j)
                g, at = a // 4, a % 4 * P
                for k in range(QT):
                    for h in range(2):
                        last = pe.matmul(otb[h * HD:(h + 1) * HD, k * P:S], v[:, g, k, at + h * HD:at + (h + 1) * HD],
                                         pt[:, h, KOFF[k]:KOFF[k] + S - k * P], start=(k == 0), stop=(k == QT - 1))
                last.then_inc(s["pv"], 1)

            def project_out(j, a):
                pe.wait_ge(s["oe"], j + 1)
                wait(pe, "ac", j)
                for t in range(QT):
                    last = pe.matmul(opb[:, t * P:(t + 1) * P], oT[:, t * P:(t + 1) * P], wo[:, a, :],
                                     start=True, stop=True)
                last.then_inc(s["op"], 1)

            def turn_h(b):
                pe.wait_ge(s["xh"], b)
                for q in range(QT):
                    last = pe.transpose(opb[:, q * P:(q + 1) * P], xh[:, q, :], ident)
                last.then_inc(s["t_h"], 1)

            def logits(b):
                pe.wait_ge(s["hh"], b)
                for q in range(QT):
                    last = pe.matmul(opb[:, q * E:(q + 1) * E], h2T[:, q * P:(q + 1) * P], wg[:, :],
                                     start=True, stop=True)
                last.then_inc(s["lg"], 1)

            def places(b):
                pe.wait_ge(s["oh"], b)
                pe.matmul(opb[:, 0:QT * E], upper16[:, :], oh16[:, :], start=True, stop=False)
                for t in range(1, QT):
                    pe.matmul(opb[:, t * E:QT * E], ones16[:, :], oh16[:, 0:(QT - t) * E],
                              start=False, stop=(t == QT - 1))
                for t in range(QT):
                    last = pe.matmul(opb[:, QT * E:(QT + 1) * E], ones16[:, :], oh16[:, t * E:(t + 1) * E],
                                     start=(t == 0), stop=(t == QT - 1))
                last.then_inc(s["pre"], 1)

            def turn(b, first, last):
                for a in range(PAIRS):
                    step(8 * b + a, a % 2, b, a, first, last)

            def step(j, par, b, a, first, last):
                before, after = not (first and a == 0), not (last and a == PAIRS - 1)
                n, m = (b, a + 1) if a + 1 < PAIRS else (b + 1, 0)
                for k in range(8):
                    scores(j, k)
                    if k == 4 and after:
                        project_q(j + 1, n, m, 0)
                    if before and k in TURN:
                        transposes(j - 1, 1 - par, *divmod(TURN.index(k), 3))
                    if k == 0 and not (first and a < 2):
                        if a == 4 and not last:
                            pe.wait_ge(s["hn"], b + 2)
                        if a in (5, 6, 7) and not first:
                            pe.wait_ge(s[("hh", "lge", "prx")[a - 5]], b)
                        project_out(j - 2, (a - 2) % PAIRS)
                    if k == 1 and not (last and V_OF[a][0]):
                        pe.wait_ge(s["qe"], 2 * j + 2)
                        if a == 5:
                            pe.wait_ge(s["vlo"], b + 2)
                        project_v(prb[1], *V_OF[a][1:])
                    if k == 4:
                        if a == 3 and not last:
                            wait(pe, "ac", j - 1)
                            turn_x(b + 1)
                        if a in (4, 5, 6) and not first:
                            wait(pe, "ac", j - 1)
                            (turn_h, logits, places)[a - 4](b)
                    if k == 5 and after:
                        project_k(j + 1, n, m)
                    if k == 7 and before:
                        weighted(j - 1, (a - 1) % PAIRS, 8 * b + 4 * ((a - 1) // 4) + 4)
                if after:
                    project_q(j + 1, n, m, 1, 8 * B if last and V_OF[a][0] else j + 4)

            pe.wait_ge(s["wo"], 16)
            pe.wait_ge(s["whi"], 5)
            pe.wait_ge(s["wlo"], 4)
            pe.wait_ge(s["wlo_k"], 1)
            project_q(0, None, 0, 0)
            project_q(0, None, 0, 1)
            project_k(0, None, 0)
            pe.wait_ge(s["wv"], 2)
            for t in range(3):
                project_v(bank[V_BANKS[t]], 0, t)
            pe.wait_ge(s["mev"], 1)
            pe.wait_ge(s["bias"], 4)
            pe.wait_ge(s["misc"], 48)
            pe.wait_ge(s["ve"], 3)
            pe.wait_ge(s["ktab"], 48)
            pe.wait_ge(s["kt"], 4)
            batches(pe, turn)
            project_out(NJ - 2, PAIRS - 2)
            for h in range(2):
                for g in range(3):
                    transposes(NJ - 1, 1, h, g)
            weighted(NJ - 1, PAIRS - 1, NJ)
            project_out(NJ - 1, PAIRS - 1)
            pe.wait_ge(s["ac"], NJ)
            turn_h(B)
            logits(B)
            pe.wait_ge(s["lge"], B)
            places(B)

            def turn_e(r):
                for t in range(ST):
                    last = pe.transpose(bank[r % 2][:, t * P:(t + 1) * P], slots[:, r % 4, t, 0:D], ident)
                last.then_inc(s["tx"], 1)

            def hidden(e, r):
                pe.wait_ge(s["xt"], e + 1)
                for n in range(NB):
                    pe.matmul(bank[2 + n][:, 0:CAP], wring[r][:, 0, n, :], qx[:, r % 2, 0:CAP],
                              start=True, stop=True).then_inc(s["hm"], 1)

            def down(e, r):
                pe.wait_ge(s["hh2"], 2 * e + 1)
                for t in range(ST):
                    for n in range(NB):
                        if t == 0:
                            pe.wait_ge(s["hr" if n % 2 == 0 else "hh2"], 2 * e + n // 2 + 1)
                        last = pe.matmul(bank[6 + r % 2][:, t * P:(t + 1) * P], hid[:, r % 2, n, t * P:(t + 1) * P],
                                         wring[r][:, 1, n, :], start=(n == 0), stop=(n == NB - 1))
                last.then_inc(s["ym"], 1)

            pe.wait_ge(s["prx"], B)
            pe.wait_ge(s["xl0"], 16)
            turn_e(0)
            with pe.Fori(0, E // 8) as g:
                for r in range(8):
                    e = 8 * g + r
                    pe.wait_ge(s[f"w{r}"], 32 * (g + 1))
                    hidden(e, r)
                    pe.wait_ge(s[f"xl{(r + 1) % 4}"], 32 * g + 16 * ((r + 1) // 4) + 16)
                    turn_e(r + 1)
                    down(e, r)

        @block.vector
        def _(dve):
            link = Chain(dve, s["dch"])
            link(dve.memset(fill[:, :], 0.0))
            dve.memset(fill[:, RW - 1:RW], float(NOWHERE)).then_inc(s["zero"], 1)
            dve.memset(ones16[:, :], 1.0).then_inc(s["zero"], 1)
            dve.memset(base[:, :], 0.0).then_inc(s["zero"], 1)
            dve.wait_ge(s["t_small"], 1)
            dve.tensor_copy(smallT[:, :], bank[0][:, 0:80]).then_inc(s["smallT"], 1)
            dve.wait_ge(s["t_pos"], 1)
            dve.wait_ge(s["posT"], 1)
            for h in range(2):
                rows = slice(h * HD, (h + 1) * HD)
                dve.tensor_copy(posT[rows, :, h, :, :], bank[1][rows, 0:PAIRS * FREQS]
                                .rearrange("p (a o f) -> p a o f", o=1, f=FREQS).to_broadcast([HD, PAIRS, 2, FREQS]))\
                    .then_inc(s["posT"], 1)
            wqT = prob[:, 0, :, :].rearrange("p a w -> p (a w)")
            for i in range(2):
                dve.wait_ge(s["t_wq"], i + 1)
                dve.tensor_copy(wqT[:, i * 512:(i + 1) * 512], bank[2 + i][:, :]).then_inc(s["wqT"], 1)

            dve.wait_ge(s["e_silu"], 1)
            link(dve.tensor_scalar(silu[:, 1, :], silu[:, 0, :], 1.0, None, ALU.add))
            link(dve.reciprocal(silu[:, 2, :], silu[:, 1, :]))
            dve.tensor_tensor(silu[:, 3, :], silu[:, 2, :], smallT[:, 8:16], ALU.mult).then_inc(s["silu"], 1)

            def moments(i):
                st, m = stats[:, i], mom[:, i]
                me, mo, ve, vo = (st[:, :, c] for c in (1, 4, 2, 5))
                yield lambda: (link(dve.tensor_tensor(m[:, 0, :], me, mo, ALU.add)),
                               link(dve.tensor_tensor(m[:, 1, :], me, mo, ALU.subtract)),
                               link(dve.tensor_tensor(m[:, 2, :], ve, vo, ALU.add)))
                yield lambda: (link(dve.tensor_tensor(m[:, 3, :], m[:, 1, :], m[:, 1, :], ALU.mult)),
                               link(dve.scalar_tensor_tensor(m[:, 1, :], m[:, 3, :], D / 4.0, m[:, 2, :],
                                                             ALU.mult, ALU.add)))
                yield lambda: (link(dve.tensor_scalar(m[:, 0, :], m[:, 0, :], 0.5, None, ALU.mult)),
                               dve.tensor_scalar(m[:, 4, :], m[:, 1, :], 1.0 / D, EPS, ALU.mult, ALU.add)
                               .then_inc(s[f"rst{i + 1}"], 1))

            def x_of(n, q):
                return x[:, bass.ds(n * QT + q, 1), :].rearrange("p a d -> p (a d)")

            def stats1(n):
                for q in range(QT):
                    end = dve.bn_stats(stats[:, 0, q, :], x_of(n, q))
                link(end)

            def xhat1(n):
                dve.wait_ge(s["rs1"], n + 1)
                for q in range(QT):
                    end = dve.tensor_scalar(xn[:, q, :], x_of(n, q), mom[:, 0, 0, q:q + 1], mom[:, 0, 5, q:q + 1],
                                            ALU.subtract, ALU.mult)
                end.then_inc(s["xn"], 1)

            def low(n):
                dve.wait_ge(s["vhi"], n + 1)
                dve.tensor_tensor(vlo[:, :], hn[:, :], vhi[:, :], ALU.subtract).then_inc(s["vlo"], 1)

            dve.wait_ge(s["x0"], 16)
            stats1(0)
            for part in moments(0):
                part()
            dve.wait_ge(s["wv"], 1)
            dve.tensor_tensor(wvlo[:, :], qkv[:, 2, :], wvhi[:, :], ALU.subtract).then_inc(s["wv"], 1)
            xhat1(0)
            dve.wait_ge(s["mod_mm"], 1)
            half = lambda c: bank[0][:, c * B:(c + 2) * B].rearrange("p (i b) -> p i b", i=2)
            dve.tensor_copy(modT[:, 0:3:2, :], half(0)).then_inc(s["modT"], 1)
            dve.tensor_scalar(modT[:, 1:4:2, :], half(2), 1.0, None, ALU.add).then_inc(s["modT"], 1)
            dve.wait_ge(s["whi"], 2)
            for h in range(2):
                cols = slice(h * P, h * P + HD)
                dve.tensor_tensor(wlo[:, :, cols], qkv[:, 0, :].rearrange("p (a h d) -> p a h d", h=2, d=HD)[:, :, h, :],
                                  whi[:, :, cols], ALU.subtract).then_inc(s["wlo"], 1)
            for i in range(2):
                dve.wait_ge(s["whi"], 4 + i)
                dve.tensor_tensor(g_of(wlo, i), bank[4 + i][:, :].rearrange("p (a h w) -> p a h w", h=2, w=HD),
                                  g_of(whi, i), ALU.subtract).then_inc(s["wlo"], 1)
            low(0)
            dve.wait_ge(s["vlo"], 1)
            dve.tensor_copy(hlo[:, 0, :], vlo[:, :]).then_inc(s["hld"], 1)
            dve.tensor_copy(mrow[:, :, :].rearrange("p a d -> p (a d)"), bank[6][0:B, :]).then_inc(s["mev"], 1)

            def scores(j, par, k):
                q = ORDER[k % QT]
                w = P * (q + 1)
                waits(dve, ("consts", 16), ("sc", 8 * j + k + 1), ("ex", 8 * j + k - 3))
                dve.tensor_tensor_reduce(out=srow[:, k % 4, 0:w], in0=scb[k % 2][:, 0:w], in1=mask[:, S - w:S],
                                         scale=-1.0, scalar=BIG, op0=ALU.add, op1=ALU.min,
                                         accum_out=nmax[:, par, k:k + 1]).then_inc(s["tt"], 1)

            def evac_pt(j, g):
                dve.wait_ge(s["tr"], 6 * j + g + 1)
                dve.tensor_copy(pt[:, 0, KOFF[g]:KOFF[g] + GW[g]], trb[g % 2][:, 0:GW[g]]).then_inc(s["evA"], 1)

            def recip(j, par, h):
                dve.wait_ge(s["ex"], 8 * j + 4 * h + 4)
                dve.reciprocal(rsum[:, par, 4 * h:4 * h + 4], sums[:, par, 4 * h:4 * h + 4]).then_inc(s["rc"], 1)

            def evac_q(j, a, h):
                dve.wait_ge(s["qp"], 2 * j + h + 1)
                dve.scalar_tensor_tensor(qx[:, h, :], prb[h][:, :], qbias[:, h, a:a + 1], qtab,
                                         ALU.add, ALU.mult).then_inc(s["qe"], 1)

            def low_k(j, h):
                dve.wait_ge(s["ke"], 2 * j + h + 1)
                dve.scalar_tensor_tensor(klo[0:HD, h, :], prb[0][h * HD:(h + 1) * HD, :], C_QKV, khi[0:HD, h, :],
                                         ALU.mult, ALU.subtract).then_inc(s["kl"], 1)

            def accumulate(j, a):
                dve.wait_ge(s["op"], j + 1)
                wait(dve, "ac", j)
                start = bo[:, None, :].to_broadcast([P, QT, D]) if a == 0 else acc[:, :, :]
                dve.tensor_tensor(acc[:, :, :], opb[:, :].rearrange("p (t d) -> p t d", t=QT), start, ALU.add)\
                    .then_inc(s["ac"], 1)

            def residual(b):
                dve.wait_ge(s["modb"], 16)
                dve.wait_ge(s["ac"], 8 * b)
                link(dve.tensor_tensor(acc[:, :, :], acc[:, :, :], one(modb, b - 1, 0).to_broadcast([P, QT, D]), ALU.mult))

            def residual2(b):
                if isinstance(b, int):
                    dve.wait_ge(s["scat"], 64 * (b - 1))
                else:
                    dve.wait_ge(s["nm"], 16 * b)
                dve.tensor_tensor(row[:, :, D:2 * D], x[:, bass.ds((b - 1) * QT, QT), :], acc[:, :, :], ALU.add)\
                    .then_inc(s["x2"], 1)

            def stats2(b):
                dve.wait_ge(s["x2"], b)
                for q in range(QT):
                    end = dve.bn_stats(stats[:, 1, q, :], row[:, q, D:2 * D])
                link(end)

            def xhat2(b):
                dve.wait_ge(s["rs2"], b)
                for q in range(QT):
                    end = dve.tensor_scalar(xh[:, q, :], row[:, q, D:2 * D], mom[:, 1, 0, q:q + 1],
                                            mom[:, 1, 5, q:q + 1], ALU.subtract, ALU.mult)
                end.then_inc(s["xh"], 1)

            te = lambda t: t.rearrange("p (t e) -> p t e", e=E)
            each = lambda t: t[:, :, None].to_broadcast([P, QT, E])
            lmax, esum, gate, emax, where, late, tmp1, tmp2 = (rsm[:, i, :] for i in range(8))

            def gating(b):
                dve.wait_ge(s["lg"], b)
                dve.tensor_tensor(te(lgt[:, 0, :]), te(opb[:, 0:QT * E]), bg[:, None, :].to_broadcast([P, QT, E]),
                                  ALU.add).then_inc(s["lge"], 1)
                dve.wait_ge(s["lge"], b)
                link(dve.tensor_reduce(lmax, te(lgt[:, 0, :]), AX.X, ALU.max))
                dve.tensor_tensor(te(lgt[:, 1, :]), te(lgt[:, 0, :]), each(lmax), ALU.subtract).then_inc(s["lm"], 1)

            def choice(b):
                dve.wait_ge(s["lm"], b)
                link(dve.scalar_tensor_tensor(te(lgt[:, 3, :]), te(lgt[:, 1, :]), 0.0,
                                              desc[:, None, :].to_broadcast([P, QT, E]), ALU.is_ge, ALU.mult))
                link(dve.tensor_reduce(emax, te(lgt[:, 3, :]), AX.X, ALU.max))
                dve.tensor_tensor(te(oh16[:, :]), te(lgt[:, 3, :]), each(emax), ALU.is_equal).then_inc(s["oh"], 1)

            def gate_of(b):
                dve.wait_ge(s["lex"], b)
                link(dve.tensor_reduce(esum, te(lgt[:, 2, :]), AX.X, ALU.add))
                dve.reciprocal(gate, esum).then_inc(s["gate"], 1)

            def place(b):
                dve.wait_ge(s["pre"], b)
                link(dve.tensor_tensor(te(lgt[:, 0, :]), te(opb[:, 0:QT * E]),
                                       base[:, None, :].to_broadcast([P, QT, E]), ALU.add))
                dve.tensor_tensor(base[:, :], base[:, :], opb[:, QT * E:(QT + 1) * E], ALU.add).then_inc(s["prx"], 1)
                dve.wait_ge(s["prx"], b)
                link(dve.tensor_tensor(lgt[:, 0, :], lgt[:, 0, :], oh16[:, :], ALU.mult))
                link(dve.tensor_reduce(where, te(lgt[:, 0, :]), AX.X, ALU.add))

            def route(b):
                link(dve.tensor_scalar(late, where, float(CAP), float(NOWHERE), ALU.is_ge, ALU.mult))
                link(dve.scalar_tensor_tensor(tmp1, emax, -float(CAP), where, ALU.mult, ALU.add))
                link(dve.scalar_tensor_tensor(tmp2, tmp1, float(E * CAP), late, ALU.add, ALU.add))

            def index(b):
                link(dve.tensor_copy(sidx[:, :], tmp2))
                dve.tensor_copy(row[:, :, 3 * D:RW], token[:, bass.ds((b - 1) * QT, QT)][:, :, None])\
                    .then_inc(s["idx"], 1)

            def modulation():
                dve.wait_ge(s["mev"], 1)
                g_, sign, size = mrow[:, 0:4:3, :], mtmp[:, 0], mtmp[:, 1]
                dve.tensor_copy(upper16[:, :], upper).then_inc(s["zero"], 1)
                link(dve.tensor_scalar(mrow[:, 2, :], mrow[:, 2, :], 1.0, None, ALU.add))
                link(dve.tensor_scalar(sign, g_, 0.0, 2.0, ALU.is_ge, ALU.mult))
                link(dve.scalar_tensor_tensor(size, sign, -1.0, g_, ALU.add, ALU.mult))
                link(dve.tensor_scalar(size, size, 0.25, None, ALU.max))
                dve.scalar_tensor_tensor(g_, sign, -1.0, size, ALU.add, ALU.mult).then_inc(s["gates"], 1)

            def extra(b, first, last):
                parts = {a: [] for a in range(PAIRS)}
                if not last:
                    n = b + 1
                    parts[0] = [lambda: stats1(n), *moments(0)]
                    parts[2] = [lambda: xhat1(n)]
                    parts[4] = [lambda: low(n)]
                if not first:
                    parts[1] = [lambda: residual(b), lambda: residual2(b), lambda: stats2(b), *moments(1)]
                    parts[2] = parts[2] + [lambda: xhat2(b)]
                    parts[5] = [lambda: gating(b), lambda: choice(b), None, lambda: gate_of(b)]
                    parts[6] = [lambda: place(b), lambda: route(b), lambda: index(b)]
                else:
                    parts[1] = [modulation]
                return parts

            def turn(b, first, last):
                parts = extra(b, first, last)
                for a in range(PAIRS):
                    step(8 * b + a, a % 2, a, first, last, parts[a])

            def step(j, par, a, first, last, parts):
                before, after = not (first and a == 0), not (last and a == PAIRS - 1)
                for k in range(8):
                    scores(j, par, k)
                    if before and k < 2:
                        evac_pt(j - 1, k)
                    if k == 3 and not (first and a < 2):
                        accumulate(j - 2, (a - 2) % PAIRS)
                    if k == 4:
                        recip(j, par, 0)
                        if after:
                            evac_q(j + 1, (a + 1) % PAIRS, 0)
                    if k >= 5 and parts:
                        part = parts.pop(0)
                        if part:
                            part()
                if after:
                    low_k(j + 1, 0)
                recip(j, par, 1)
                if after:
                    low_k(j + 1, 1)
                    evac_q(j + 1, (a + 1) % PAIRS, 1)
                for part in parts:
                    if part:
                        part()

            dve.wait_ge(s["misc"], 48)
            dve.wait_ge(s["bias"], 4)
            dve.wait_ge(s["x1"], 16)
            evac_q(0, 0, 0)
            evac_q(0, 0, 1)
            for h in range(2):
                low_k(0, h)
            batches(dve, turn, lambda i: link.enter(i, LINKS), link.leave)
            accumulate(NJ - 2, PAIRS - 2)
            for g in range(2):
                evac_pt(NJ - 1, g)
            accumulate(NJ - 1, PAIRS - 1)
            for part in (residual, residual2, stats2):
                part(B)
            for part in moments(1):
                part()
            for part in (xhat2, gating, choice, gate_of, place, route, index):
                part(B)

            def expert(e, r, first=False):
                par = r % 2
                if not first:
                    dve.wait_ge(s[f"ysc{par}"], 16 * (e - par))
                for n in range(1, NB, 2):
                    dve.wait_ge(s["hm"], NB * e + n + 1)
                    dve.tensor_scalar(hid[:, par, n, :], bank[2 + n][:, 0:CAP], smallT[:, bass.ds(16 + NB * e + n, 1)],
                                      0.0, ALU.add, ALU.max).then_inc(s["hh2"], 1)
                dve.tensor_copy(yidx[:, par, :], slots[:, r, :, 3 * D]).then_inc(s["yi"], 1)
                dve.wait_ge(s["ym"], e + 1)
                rows = ye[:, par, :, :]
                link(dve.tensor_tensor(rows, bank[6 + par][:, 0:CAP].rearrange("p (t d) -> p t d", t=ST),
                                       one(b2, e, slice(None)).to_broadcast([P, ST, D]), ALU.add))
                link(dve.tensor_tensor(rows, rows, slots[:, r, :, 2 * D:3 * D], ALU.mult))
                dve.tensor_tensor(rows, rows, slots[:, r, :, D:2 * D], ALU.add).then_inc(s["y"], 1)

            dve.wait_ge(s["scat"], 64 * B)
            dve.wait_ge(s["b2"], 16)
            for e in range(4):
                expert(e, e, e < 2)
            with dve.Fori(1, E // 4) as g:
                link.enter(g - 1, 8)
                for r in range(4):
                    expert(4 * g + r, r)
            link.leave(E // 4 - 1)


def host_constants():
    k = np.arange(S, dtype=np.float64)
    f = np.arange(FREQS)
    inv = 1250.0 ** (-(f // 2 * 2) / FREQS)
    ang = inv[:, None] * k[None, :]
    even = (f % 2 == 0)[:, None]
    sig = np.sqrt(2.0) * FREQS ** -0.5
    cq = C_QKV * HD ** -0.5
    qtab = np.concatenate([np.full((HD, S), cq),
                           cq * sig * np.where(even, np.sin(ang), np.cos(ang)),
                           cq * sig * np.where(even, -np.cos(ang), np.sin(ang))])
    ktab = np.concatenate([np.cos(ang), np.sin(ang)])
    causal = np.where(np.arange(P)[None, :] > np.arange(P)[:, None], NEG, 0.0)
    mask = np.concatenate([np.zeros((P, S - P)), causal], axis=1)
    desc = np.broadcast_to(E - np.arange(E), (P, E))
    upper = (np.arange(P)[:, None] < np.arange(P)[None, :]).astype(np.float64)
    token = (np.arange(P)[:, None] + P * np.arange(TILES)[None, :]).astype(np.float64)
    consts = np.concatenate([np.eye(P), mask, qtab, desc, upper, token], axis=1)
    return np.ascontiguousarray(consts, dtype=np.float32), np.ascontiguousarray(ktab, dtype=np.float32)


NAMES = ["L0_attn_input", "L0_attn_qkv", "L0_attn_q_bias", "L0_attn_positional", "L0_attn_out_kernel",
         "L0_attn_out_bias", "L0_ffn_Wg", "L0_ffn_bg", "L0_ffn_W1", "L0_ffn_b1", "L0_ffn_W2", "L0_ffn_b2",
         "L0_c", "L0_wmod"]


def kernel(**inputs):
    import concourse.bacc as bacc
    from concourse.bass_utils import run_bass_kernel_spmd

    nc = bacc.Bacc("TRN2", target_bir_lowering=False, num_devices=1)
    arrays, args = {}, []
    consts, ktab = host_constants()
    for name, a in [(n, np.ascontiguousarray(inputs[n])) for n in NAMES] + [("consts", consts), ("ktab", ktab)]:
        arrays[f"in_{name}"] = a
        args.append(nc.dram_tensor(f"in_{name}", a.shape, mybir.dt.from_np(a.dtype), kind="ExternalInput").ap())
    out = nc.dram_tensor("out_0", (B, S, D), F32, kind="ExternalOutput").ap()
    program(nc, *args, out)
    r = run_bass_kernel_spmd(nc, [arrays], core_ids=[0])
    return r.results[0]["out_0"]
```

```python
from contextlib import ExitStack

import numpy as np
import concourse.bass as bass
from concourse import mybir

F32 = mybir.dt.float32
F32R = mybir.dt.float32r
BF16 = mybir.dt.bfloat16
U32 = mybir.dt.uint32
ALU = mybir.AluOpType
ACT = mybir.ActivationFunctionType
AX = mybir.AxisListType

P = 128
B, S, D = 8, 512, 128
HEADS, HD, FREQS = 16, 64, 32
PAIRS = HEADS // 2
NJ = B * PAIRS
TILES = B * S // P
QT = S // P
E, FF = 16, 512
CAP = B * S // E
NB = FF // P
ST = CAP // P
EPS = 1e-5
C_QKV = (3.0 * D * HD * HEADS) ** -0.25
C_OUT = (HEADS * HD * D) ** -0.25
NEG = -1e30
BIG = 3e38
WP = 2 * P + P
RW = 3 * D + 1
NOWHERE = 8 * B * S
LINKS = 25
GW = [S, 384, 384]
GROUPS = [[(q, 0) for q in range(4)], [(q, 1) for q in range(1, 4)], [(2, 2), (3, 2), (3, 3)]]
QOFF = [0, 128, 384, 768]
KOFF = [0, 512, 896, 1152]
PW = 1280
V_OF = [(0, 0, 3)] + [(0, 1, t) for t in range(4)] + [(1, 0, t) for t in range(3)]
V_BANKS = [2, 3, 0]
KLO = 1
TURN = [0, 1, 2, 3, 4, 5]
ORDER = [3, 2, 1, 0]


def program(nc, x_d, qkv_d, qb_d, pos_d, wo_d, bo_d, wg_d, bg_d, w1_d, b1_d, w2_d, b2_d, c_d, wmod_d,
            consts_d, ktab_d, out_d):
    ctx = ExitStack()
    with ctx:
        def sb(name, shape, dt=F32):
            return ctx.enter_context(nc.sbuf_tensor(name, shape, dt))

        def sem(name):
            return ctx.enter_context(nc.semaphore(name))

        x = sb("x", [P, TILES, D])
        acc = sb("acc", [P, S])
        modb = sb("modb", [P, B, 3, D])
        whi = sb("whi", [P, PAIRS, WP], F32R)
        wlo = sb("wlo", [P, PAIRS, WP], F32R)
        wvhi = sb("wvhi", [P, HEADS * HD], F32R)
        wvlo = sb("wvlo", [P, HEADS * HD], F32R)
        raw = sb("raw", [P, 4 * HEADS * HD])
        qkv = raw[:, 0:3 * HEADS * HD].rearrange("p (i w) -> p i w", i=3)
        pos = raw[0:FREQS, 3 * HEADS * HD:]
        wohi = sb("wohi", [P, PAIRS, D], F32R)
        wolo = sb("wolo", [P, PAIRS, D], F32R)
        wmod = sb("wmod", [P, 6, D])
        consts = sb("consts", [P, 128 + 512 + 512 + 16 + 128 + TILES])
        ident = consts[:, 0:128]
        mask = consts[:, 128:640]
        qtab = consts[:, 640:1152]
        desc = consts[:, 1152:1168]
        upper = consts[:, 1168:1296]
        token = consts[:, 1296:1296 + TILES]
        small = sb("small", [80, P])
        smallT = sb("smallT", [P, 80])
        qbias = sb("qbias", [P, 2, PAIRS])
        posT = sb("posT", [P, PAIRS, 2, 2, FREQS])
        wg = sb("wg", [P, E])
        bg = sb("bg", [P, E])
        bo = sb("bo", [P, 1])
        silu = sb("silu", [P, 4, B])
        mrow = sb("mrow", [B, 3, D])
        gtmp = sb("gtmp", [P, 2, B])
        modT = sb("modT", [P, 5, B])
        stats = sb("stats", [P, 2, QT, 6])
        mom = sb("mom", [P, 2, 6, QT])
        mhalf = sb("mhalf", [P, QT])
        hn = sb("hn", [P, S])
        vhi = sb("vhi", [P, S], F32R)
        vlo = sb("vlo", [P, S], F32R)
        hhi = sb("hhi", [P, 2, S], F32R)
        hlo = sb("hlo", [P, 2, S], F32R)
        row = sb("row", [P, QT, RW])
        wo = row[:, :, :].rearrange("p t w -> p (t w)")[:, 0:PAIRS * D].rearrange("p (a d) -> p a d", d=D)
        fill = sb("fill", [P, RW])
        h2T = sb("h2T", [P, S])
        xh = sb("xh", [P, QT, D])
        xn = xh
        mtmp = xh[0:B, 0:2, :]
        lgt = sb("lgt", [P, 5, QT * E])
        oh16 = sb("oh16", [P, QT * E], BF16)
        rsm = sb("rsm", [P, 10, QT])
        base = sb("base", [P, E])
        sidx = sb("sidx", [P, QT], U32)
        upper16 = sb("upper16", [P, P], BF16)
        ones16 = sb("ones16", [P, P], BF16)
        qx = sb("qx", [P, 2, S])
        qhi = sb("qhi", [P, 2, S - P], F32R)
        qlo = sb("qlo", [P, 2, S - P], F32R)
        kx = sb("kx", [P, 2, P])
        khi = sb("khi", [P, 2, S], F32R)
        klo = sb("klo", [P, 2, S], F32R)
        v = sb("v", [P, 2, QT, S])
        srow = sb("srow", [P, 4, S])
        nmax = sb("nmax", [P, 2, 8])
        sums = sb("sums", [P, 2, 8])
        rsum = sb("rsum", [P, 2, 8])
        prob = sb("prob", [P, 2, 2, PW])
        pt = sb("pt", [P, 2, PW])
        ohi = sb("ohi", [P, S], F32R)
        olo = sb("olo", [P, S], F32R)
        w1 = raw[:, :].rearrange("p (r n d) -> p r n d", r=8, n=NB)
        w2 = prob[:, :, :, :].rearrange("p a b w -> p (a b w)")[:, 0:8 * NB * D] \
            .rearrange("p (r n d) -> p r n d", r=8, n=NB)
        w1hi, w1lo = (t[:, :, :].rearrange("p a w -> p (a w)")[:, 0:2 * NB * P]
                      .rearrange("p (i n d) -> p i n d", i=2, n=NB) for t in (whi, wlo))
        xhi, xlo = (t[:, :, 0:CAP] for t in (hhi, hlo))
        b2 = v[:, 0, :, :].rearrange("p t s -> p (t s)").rearrange("p (e d) -> p e d", e=E)
        xf = x[:, :, :].rearrange("p t d -> p (t d)")
        slots = xf[:, 0:4 * ST * RW].rearrange("p (a t w) -> p a t w", a=4, t=ST)
        hid = srow[:, :, :].rearrange("p k s -> p (k s)").rearrange("p (a n c) -> p a n c", a=2, n=NB)
        ye = row[:, :, 0:D].rearrange("p (a t) d -> p a t d", a=2)
        yidx = sb("yidx", [P, 2, ST], U32)
        bank = [ctx.enter_context(nc.psum_tensor(f"bank{i}", [P, 512], F32)) for i in range(8)]
        scb, trb, prb, otb, opb = bank[0:2], bank[2:4], bank[4:6], bank[6], bank[7]
        free = [*trb, *prb, *scb]
        xbuf = nc.dram_tensor("xbuf", [E * CAP, RW], F32).ap()
        mod_dram = nc.dram_tensor("mod_rows", [B, 3 * D], F32).ap()

        names = ("ident consts small pos w_q w_k w_v ktab x0 x1 wmod misc b2 wo zero "
                 "t_small smallT e_silu silu t_pos posT t_wq wqT wg_mm bias whi wlo wlo_k mod_mm modT mev mrow modb gates "
                 "st rst1 rs1 xn t_x hn vhi vlo hld wv qh ql kl kt wos ol ga t_a "
                 "sc tt ex rc nm tr evA evB pv oe qp qe kp ke vp ve op ac "
                 "dch pch x2 rst2 rs2 xh h2a h2 t_h hh lg lge lm lex oh gate gg pre prx idx scat filled x2st "
                 "xl0 xl1 xl2 xl3 w0 w1 w2 w3 w4 w5 w6 w7 w1h w1l tx xt xl hm hr hh2 ym y yi ysc0 ysc1").split()
        s = {n: sem("s_" + n) for n in names}

        class Chain:

            def __init__(self, eng, semaphore):
                self.eng, self.sem, self.base, self.n = eng, semaphore, 0, 0

            def __call__(self, ins):
                self.n += 1
                ins.then_inc(self.sem, 1)
                self.eng.wait_ge(self.sem, self.base + self.n)

            def enter(self, turns, per):
                self.before, self.per = self.base + self.n, per
                self.base, self.n = self.before + per * turns, 0

            def leave(self, turns):
                assert self.n == self.per, self.n
                self.base, self.n = self.before + self.per * turns, 0

        def wait(eng, name, value):
            if not isinstance(value, int) or value > 0:
                eng.wait_ge(s[name], value)

        def waits(eng, *pairs):
            values = [v if isinstance(v, int) else eng.compute_val(v) for _, v in pairs]
            for (name, _), v in zip(pairs, values):
                wait(eng, name, v)

        def batches(eng, turn, enter=None, leave=None):
            turn(0, True, False)
            with eng.Fori(1, B - 1) as b:
                if enter:
                    enter(b - 1)
                turn(b, False, False)
            if leave:
                leave(B - 2)
            turn(B - 1, False, True)

        def g_of(tile, i):
            return tile[:, 4 * i:4 * i + 4, 0:2 * P].rearrange("p a (h c) -> p a h c", h=2)[:, :, :, HD:P]

        def one(tile, b, *rest):
            return tile[(slice(None), bass.ds(b, 1)) + rest]

        block = ctx.enter_context(nc.Block())

        @block.sync
        def _(sp):
            sp.dma_start(ident, consts_d[:, 0:128]).then_inc(s["ident"], 16)
            sp.dma_start(small[0:8, :], qb_d.rearrange("(a h) d -> a (h d)", h=2)).then_inc(s["small"], 16)
            sp.dma_start(small[8:16, :], c_d).then_inc(s["small"], 16)
            sp.dma_start(small[16:80, :], b1_d.rearrange("e (n p) -> (e n) p", p=P)).then_inc(s["small"], 16)
            xt_d = x_d.rearrange("b (t p) d -> p (b t) d", p=P)
            sp.dma_start(x[:, 0:QT, :], xt_d[:, 0:QT, :]).then_inc(s["x0"], 16)
            sp.dma_start(wmod[:, :, :], wmod_d.rearrange("p (a b) -> p a b", a=6)).then_inc(s["wmod"], 16)
            sp.dma_start(consts[:, 128:], consts_d[:, 128:]).then_inc(s["consts"], 16)
            for h in range(2):
                sp.dma_start(kx[HD:P, h, :], ktab_d[:, 0:P]).then_inc(s["ktab"], 16)
            sp.dma_start(h2T[HD:P, :], ktab_d).then_inc(s["ktab"], 16)
            sp.dma_start(bo[:, :], bo_d.rearrange("(p a) -> p a", a=1)).then_inc(s["misc"], 16)
            sp.dma_start(wg[:, :], wg_d).then_inc(s["misc"], 16)
            sp.dma_start(bg[:, :], bg_d.rearrange("(a n) -> a n", a=1).to_broadcast([P, E])).then_inc(s["misc"], 16)
            sp.dma_start(x[:, QT:TILES, :], xt_d[:, QT:TILES, :]).then_inc(s["x1"], 16)
            sp.dma_start(wo[:, :, :], wo_d.rearrange("(a p) d -> p a d", p=P)).then_inc(s["wo"], 16)
            out_v = out_d.rearrange("b (t p) d -> p b t d", p=P)

            def load_w1(e, slot):
                sp.dma_start(w1[:, slot, :, :], w1_d[e].rearrange("p (n d) -> p n d", n=NB))\
                    .then_inc(s[f"w{slot}"], 16)

            def load_w2(e, slot):
                sp.dma_start(w2[:, slot, :, :], w2_d[e].rearrange("(n p) d -> p n d", p=P))\
                    .then_inc(s[f"w{slot}"], 16)

            def rows(e, slot):
                sp.dma_start(slots[:, slot, :, :], xbuf.rearrange("(e t p) w -> e p t w", p=P, t=ST)[e])\
                    .then_inc(s[f"xl{slot}"], 16)

            def at(value):
                return value if isinstance(value, int) else sp.compute_val(value)

            def turn(b, first, last):
                if first:
                    sp.wait_ge(s["gates"], 2)
                    sp.dma_start(mod_dram, mrow[:, :, :].rearrange("p a d -> p (a d)")).then_inc(s["mrow"], 16)
                    sp.wait_ge(s["mrow"], 16)
                    sp.dma_start(modb[:, :, :, :].rearrange("p b a d -> p (b a d)"),
                                 mod_dram.rearrange("(o b) w -> o (b w)", o=1).to_broadcast([P, B * 3 * D]))\
                        .then_inc(s["modb"], 16)
                    sp.wait_ge(s["zero"], 2)
                    for q in range(4):
                        sp.dma_start(xbuf.rearrange("(p r) w -> p r w", p=P)[:, 8 * q:8 * q + 8, :],
                                     fill[:, None, :].to_broadcast([P, 8, RW])).then_inc(s["filled"], 16)
                    sp.wait_ge(s["wlo_k"], 1)
                    sp.wait_ge(s["wlo"], 4)
                    sp.wait_ge(s["wv"], 2)
                    sp.wait_ge(s["t_wq"], 2)
                    sp.wait_ge(s["t_pos"], 1)
                    for e in range(8):
                        load_w1(e, e)
                else:
                    store(b)

            def store(b):
                p = at(b - 1)
                sp.wait_ge(s["x2"], b)
                sp.dma_start(out_v[:, bass.ds(p, 1), :, :].rearrange("p a t d -> p (a t) d"),
                             row[:, :, D:2 * D]).then_inc(s["x2st"], 16)

            batches(sp, turn)
            store(B)
            sp.wait_ge(s["pv"], NJ)
            for e in range(8):
                load_w2(e, e)
            sp.dma_start(b2, b2_d.rearrange("(a e) d -> a e d", a=1).to_broadcast([P, E, D])).then_inc(s["b2"], 16)
            sp.wait_ge(s["scat"], 64 * B)
            for e in range(4):
                rows(e, e)
            for e in range(E - 3):
                if e < E - 8:
                    sp.wait_ge(s["ym"], e + 1)
                    load_w1(e + 8, e)
                    load_w2(e + 8, e)
                sp.wait_ge(s["y"], e + 1)
                rows((e + 4) % E, e % 4)

        @block.gpsimd
        def _(gp):
            def rstd(i, n):
                waits(gp, ("pch", 1), (f"rst{i + 1}", n))
                gp.tensor_tensor(mom[:, i, 5, :], mom[:, i, 4, :], mhalf[:, :], ALU.pow).then_inc(s[f"rs{i + 1}"], 1)

            gp.memset(posT[:, :, :, :, :], 0.0).then_inc(s["posT"], 1)
            gp.memset(mhalf[:, :], -0.5).then_inc(s["pch"], 1)
            gp.wait_ge(s["pch"], 1)
            rstd(0, 1)
            gp.wait_ge(s["w_k"], 16)
            gp.wait_ge(s["whi"], 3)
            gp.tensor_tensor(wlo[:, :, 2 * P:3 * P], qkv[:, 1, :].rearrange("p (a w) -> p a w", a=PAIRS),
                             whi[:, :, 2 * P:3 * P], ALU.subtract).then_inc(s["wlo_k"], 1)
            gp.wait_ge(s["wlo_k"], 1)
            gp.wait_ge(s["kt"], 2)
            for h in range(2):
                gp.tensor_tensor(klo[HD:P, h, :], h2T[HD:P, :], khi[HD:P, h, :], ALU.subtract).then_inc(s["kt"], 1)
            gp.wait_ge(s["kt"], 4)

            def copy(n, i):
                half = gp.compute_val(n & 1) if not isinstance(n, int) else n & 1
                waits(gp, ("pch", 1), ("vhi", n + 1), ("vlo", n + 1))
                there, here = ((hhi, vhi), (hlo, vlo))[i]
                gp.tensor_copy(there[:, bass.ds(half, 1), :].rearrange("p a s -> p (a s)"), here[:, :])\
                    .then_inc(s["hld"], 1)

            def modulate(b):
                p = gp.compute_val(b - 1) if not isinstance(b, int) else b - 1
                waits(gp, ("modb", 16), ("xh", b))
                gp.tensor_tensor(row[:, :, 0:D], xh[:, :, :], one(modb, p, 1).to_broadcast([P, QT, D]), ALU.mult)\
                    .then_inc(s["h2a"], 1)
                gp.wait_ge(s["h2a"], b)
                gp.tensor_tensor(row[:, :, 0:D], row[:, :, 0:D], one(modb, p, 0).to_broadcast([P, QT, D]), ALU.add)\
                    .then_inc(s["h2"], 1)

            def gated(b):
                p = gp.compute_val(b - 1) if not isinstance(b, int) else b - 1
                waits(gp, ("modb", 16), ("gate", b))
                gp.tensor_tensor(row[:, :, 2 * D:3 * D], rsm[:, 2, :, None].to_broadcast([P, QT, D]),
                                 one(modb, p, 2).to_broadcast([P, QT, D]), ALU.mult).then_inc(s["gg"], 1)

            def scatter(b):
                waits(gp, ("filled", 64), ("gg", b), ("h2", b), ("idx", b), ("x2st", 16 * b))
                for t in range(QT):
                    gp.indirect_dma_start(out=xbuf, out_offset=bass.IndirectOffsetOnAxis(ap=sidx[:, t:t + 1], axis=0),
                                          in_=row[:, t, :], in_offset=None,
                                          bounds_check=E * CAP - 1, oob_is_err=False).then_inc(s["scat"], 16)

            def low_q(j, h):
                waits(gp, ("pch", 1), ("qh", 2 * j + h + 1))
                gp.tensor_tensor(qlo[:, h, :], qx[:, h, P:S], qhi[:, h, :], ALU.subtract).then_inc(s["ql"], 1)

            def divide(j, par, h, *others):
                waits(gp, ("pch", 1), ("rc", 2 * j + h + 1), *others)
                for q in range(QT):
                    part = prob[:, par, h, QOFF[q]:QOFF[q] + P * (q + 1)]
                    end = gp.tensor_scalar(part, part, rsum[:, par, 4 * h + q:4 * h + q + 1], 1.0,
                                           ALU.mult, ALU.mult)
                end.then_inc(s["nm"], 1)

            def turn(b, first, last):
                for a in range(PAIRS):
                    j = 8 * b + a
                    low_q(j, 1)
                    if not last:
                        if a == 1:
                            rstd(0, b + 2)
                        if a in (5, 6):
                            copy(b + 1, a - 5)
                    if not first:
                        if a == 3:
                            rstd(1, b)
                        if a == 4:
                            modulate(b)
                        if a == 6:
                            gated(b)
                        if a == 7:
                            scatter(b)
                    divide(j, a % 2, 0)
                    if not (last and a == PAIRS - 1):
                        low_q(j + 1, 0)
                    divide(j, a % 2, 1, *([("scat", 64 * b)] if a == 7 and not first else []))

            low_q(0, 0)
            batches(gp, turn)
            rstd(1, B)
            modulate(B)
            gated(B)
            scatter(B)

            def expert(e, par):
                waits(gp, ("pch", 1), ("y", e + 1), ("yi", e + 1))
                for t in range(ST):
                    gp.indirect_dma_start(out=out_d.rearrange("b s d -> (b s) d"),
                                          out_offset=bass.IndirectOffsetOnAxis(ap=yidx[:, par, t:t + 1], axis=0),
                                          in_=ye[:, par, t, :], in_offset=None,
                                          bounds_check=B * S - 1, oob_is_err=False).then_inc(s[f"ysc{par}"], 16)

            with gp.Fori(0, E // 2) as g:
                expert(2 * g, 0)
                expert(2 * g + 1, 1)
            for par in range(2):
                gp.wait_ge(s[f"ysc{par}"], 16 * ST * E // 2)

        @block.scalar
        def _(act):
            act.dma_start(pos[:, :], pos_d.rearrange("f n d -> f (n d)")).then_inc(s["pos"], 16)
            for i in range(3):
                act.dma_start(qkv[:, i, :], qkv_d.rearrange("p a n d -> p a (n d)")[:, i, :]).then_inc(s[f"w_{'qkv'[i]}"], 16)
            act.wait_ge(s["smallT"], 1)
            act.activation(silu[:, 0, :], smallT[:, 8:16], ACT.Exp, scale=-1.0).then_inc(s["e_silu"], 1)
            act.wait_ge(s["w_q"], 16)
            for h in range(2):
                act.activation(whi[:, :, h * P:h * P + HD],
                               qkv[:, 0, :].rearrange("p (a h d) -> p a h d", h=2, d=HD)[:, :, h, :], ACT.Copy)\
                    .then_inc(s["whi"], 1)
            act.wait_ge(s["w_k"], 16)
            act.activation(whi[:, :, 2 * P:3 * P], qkv[:, 1, :].rearrange("p (a w) -> p a w", a=PAIRS), ACT.Copy)\
                .then_inc(s["whi"], 1)
            act.wait_ge(s["w_v"], 16)
            act.activation(wvhi[:, :], qkv[:, 2, :], ACT.Copy).then_inc(s["wv"], 1)
            act.wait_ge(s["ktab"], 48)
            for h in range(2):
                act.activation(khi[HD:P, h, :], h2T[HD:P, :], ACT.Copy).then_inc(s["kt"], 1)
            for i in range(2):
                act.wait_ge(s["wg_mm"], i + 1)
                act.activation(g_of(whi, i), bank[4 + i][:, :].rearrange("p (a h w) -> p a h w", h=2, w=HD), ACT.Copy)\
                    .then_inc(s["whi"], 1)
            act.wait_ge(s["wg_mm"], 3)
            for h in range(2):
                act.activation(qbias[HD:P, h, :], bank[1][HD:P, 480 + h * PAIRS:480 + (h + 1) * PAIRS], ACT.Copy,
                               scale=1.0 / C_QKV).then_inc(s["bias"], 1)
                act.activation(qbias[0:HD, h, :], smallT[h * HD:(h + 1) * HD, 0:PAIRS], ACT.Copy,
                               scale=1.0 / C_QKV).then_inc(s["bias"], 1)

            def normed(n):
                act.wait_ge(s["t_x"], n + 1)
                wait(act, "vlo", n)
                act.activation(hn[:, :], opb[:, :], ACT.Identity, bias=modT[:, 0, bass.ds(n, 1)],
                               scale=modT[:, 1, bass.ds(n, 1)]).then_inc(s["hn"], 1)

            def high(n):
                act.wait_ge(s["hn"], n + 1)
                wait(act, "vp", 8 * n)
                wait(act, "hld", 2 * n)
                act.activation(vhi[:, :], hn[:, :], ACT.Copy).then_inc(s["vhi"], 1)

            def evac_k(j, h):
                act.wait_ge(s["kp"], j + 1)
                act.activation(khi[0:HD, h, :], prb[0][h * HD:(h + 1) * HD, :], ACT.Copy, scale=C_QKV)
                act.activation(kx[0:HD, h, :], prb[0][h * HD:(h + 1) * HD, 0:P], ACT.Copy, scale=C_QKV)\
                    .then_inc(s["ke"], 1)

            def high_q(j, h):
                act.wait_ge(s["qe"], 2 * j + h + 1)
                act.activation(qhi[:, h, :], qx[:, h, P:S], ACT.Copy).then_inc(s["qh"], 1)

            def evac_v(j, a):
                act.wait_ge(s["vp"], j + 4)
                n, g, t = V_OF[a]
                act.activation(v[:, g, t, :], prb[1][:, :], ACT.Copy).then_inc(s["ve"], 1)

            def exps(j, par, k):
                h, q = k // QT, ORDER[k % QT]
                act.wait_ge(s["tt"], 8 * j + k + 1)
                act.activation(prob[:, par, h, QOFF[q]:QOFF[q] + P * (q + 1)], srow[:, k % 4, 0:P * (q + 1)],
                               ACT.Exp, bias=nmax[:, par, k:k + 1], scale=-1.0,
                               accum_out=sums[:, par, 4 * h + q:4 * h + q + 1]).then_inc(s["ex"], 1)

            def evac_pt(j, i, source=None):
                act.wait_ge(s["tr"], 6 * j + i + 1)
                h, g = divmod(i, 3)
                source = trb[i % 2] if source is None else source
                act.activation(pt[:, h, KOFF[g]:KOFF[g] + GW[g]], source[:, 0:GW[g]], ACT.Copy)\
                    .then_inc(s["evB"], 1)

            def evac_o(j):
                act.wait_ge(s["pv"], j + 1)
                act.activation(ohi[:, :], otb[:, :], ACT.Copy, scale=C_QKV * C_OUT).then_inc(s["oe"], 1)

            def second(b):
                act.wait_ge(s["t_h"], b)
                act.activation(h2T[:, :], opb[:, :], ACT.Identity, bias=modT[:, 2, bass.ds(b - 1, 1)],
                               scale=modT[:, 3, bass.ds(b - 1, 1)]).then_inc(s["hh"], 1)

            def gates(b):
                act.wait_ge(s["lm"], b)
                act.activation(lgt[:, 2, :], lgt[:, 1, :], ACT.Exp).then_inc(s["lex"], 1)

            def turn(b, first, last):
                for a in range(PAIRS):
                    step(8 * b + a, a % 2, b, a, first, last)

            def step(j, par, b, a, first, last):
                before, after = not (first and a == 0), not (last and a == PAIRS - 1)
                high_q(j, 1)
                for k in range(8):
                    if before and k == 5:
                        evac_pt(j - 1, 5)
                    exps(j, par, k)
                    if before and k == 0:
                        evac_pt(j - 1, 1)
                    if k == 1 and not (last and V_OF[a][0]):
                        evac_v(j, a)
                    if before and 2 <= k < 5:
                        evac_pt(j - 1, k)
                    if k == 4:
                        if a == 3 and not last:
                            normed(b + 1)
                        if a == 4 and not first:
                            second(b)
                    if k == 2 and a == 4 and not last:
                        high(b + 1)
                    if after and k == 5:
                        high_q(j + 1, 0)
                        evac_k(j + 1, 0)
                    if k == 6 and a == 5 and not first:
                        gates(b)
                if after:
                    evac_k(j + 1, 1)
                if before:
                    evac_o(j - 1)

            act.wait_ge(s["modT"], 2)
            normed(0)
            high(0)
            act.wait_ge(s["vhi"], 1)
            act.activation(hhi[:, 0, :], vhi[:, :], ACT.Copy).then_inc(s["hld"], 1)
            high_q(0, 0)
            for h in range(2):
                evac_k(0, h)
            act.wait_ge(s["wo"], 16)
            act.activation(wohi[:, :, :], wo, ACT.Copy).then_inc(s["wos"], 1)
            for t in range(3):
                act.wait_ge(s["vp"], t + 1)
                act.activation(v[:, 0, t, :], bank[V_BANKS[t]][:, :], ACT.Copy).then_inc(s["ve"], 1)
            batches(act, turn)
            for i in (1, 3, 5):
                evac_pt(NJ - 1, i, free[i])
            evac_o(NJ - 1)
            second(B)
            gates(B)

            def high_w1(r, loads):
                act.wait_ge(s[f"w{r}"], 32 * loads)
                act.activation(w1hi[:, r % 2, :, :], w1[:, r, :, :], ACT.Copy).then_inc(s["w1h"], 1)

            def high_x(e, par):
                act.wait_ge(s["tx"], e + 1)
                act.activation(xhi[:, par, :], bank[par][:, 0:CAP], ACT.Copy).then_inc(s["xt"], 1)

            for r in range(2):
                high_w1(r, 1)
            high_x(0, 0)
            with act.Fori(0, E // 8) as g:
                for r in range(8):
                    e, par = 8 * g + r, r % 2
                    for n in range(0, NB, 2):
                        act.wait_ge(s["hm"], NB * e + n + 1)
                        act.activation(hid[:, par, n, :], bank[2 + n][:, 0:CAP], ACT.Relu,
                                       bias=smallT[:, bass.ds(16 + NB * e + n, 1)]).then_inc(s["hr"], 1)
                    high_x(e + 1, 1 - par)
                    act.wait_ge(s["hm"], NB * e + NB)
                    high_w1((r + 2) % 8, g + 1 if r < 6 else 2)

        @block.tensor
        def _(pe):
            pe.wait_ge(s["ident"], 16)
            pe.wait_ge(s["small"], 48)
            pe.transpose(bank[0][:, 0:80], small[:, :], ident[0:80, 0:80]).then_inc(s["t_small"], 1)
            pe.wait_ge(s["pos"], 16)
            for a in range(PAIRS):
                last = pe.transpose(bank[1][:, a * FREQS:(a + 1) * FREQS], pos[:, a * P:(a + 1) * P],
                                    ident[0:FREQS, 0:FREQS])
            last.then_inc(s["t_pos"], 1)
            pe.wait_ge(s["w_q"], 16)
            for a in range(PAIRS):
                last = pe.transpose(bank[2 + a // 4][:, (a % 4) * P:(a % 4 + 1) * P], qkv[:, 0, a * P:(a + 1) * P],
                                    ident)
                if a % 4 == 3:
                    last.then_inc(s["t_wq"], 1)
            wqT = prob[:, 0, :, :].rearrange("p a w -> p (a w)")[:, 0:PAIRS * P]
            pe.wait_ge(s["posT"], 3)
            for a in range(PAIRS):
                pe.wait_ge(s["wqT"], 1 + a // 4)
                last = pe.matmul(bank[4 + a // 4][:, (a % 4) * P:(a % 4 + 1) * P], wqT[:, a * P:(a + 1) * P],
                                 posT[:, a, :, :, :].rearrange("p h i f -> p (h i f)"), start=True, stop=True)
                if a % 4 == 3:
                    last.then_inc(s["wg_mm"], 1)
            pe.wait_ge(s["silu"], 1)
            pe.wait_ge(s["wmod"], 16)
            for i, m in enumerate((0, 3, 1, 4, 2)):
                pe.matmul(bank[0][:, i * B:(i + 1) * B], wmod[:, m, :], silu[:, 3, :], start=True, stop=True)
            pe.matmul(bank[6][0:B, 0:3 * D], silu[:, 3, :], wmod[:, 3:6, :].rearrange("p a d -> p (a d)"),
                      start=True, stop=True).then_inc(s["mod_mm"], 1)
            pe.wait_ge(s["smallT"], 1)
            for h in range(2):
                for a in range(PAIRS):
                    last = pe.matmul(bank[1][HD:P, 480 + h * PAIRS + a:481 + h * PAIRS + a],
                                     posT[:, a, h, :, :].rearrange("p i f -> p (i f)"),
                                     smallT[:, a:a + 1], start=True, stop=True)
            last.then_inc(s["wg_mm"], 1)

            def turn_x(n):
                pe.wait_ge(s["xn"], n + 1)
                for q in range(QT):
                    last = pe.transpose(opb[:, q * P:(q + 1) * P], xn[:, q, :], ident)
                last.then_inc(s["t_x"], 1)

            turn_x(0)

            def project(out, a, cols, n, name):
                if n is None:
                    hi, lo = vhi[:, :], vlo[:, :]
                else:
                    hi, lo = (t[:, bass.ds(n & 1, 1), :].rearrange("p a s -> p (a s)") for t in (hhi, hlo))
                for i, (w, h) in enumerate(((whi, hi), (whi, lo), (wlo, hi))):
                    last = pe.matmul(out, w[:, a, cols], h, start=(i == 0), stop=(i == 2))
                last.then_inc(s[name], 1)

            def project_q(j, n, a, h, ve=0):
                if n is None:
                    pe.wait_ge(s["vlo"], 1)
                elif h == 0:
                    pe.wait_ge(s["hld"], 2 * (n + 1))
                else:
                    wait(pe, "ve", ve)
                project(prb[h][:, :], a, slice(h * P, (h + 1) * P), n, "qp")

            def project_k(j, n, a):
                pe.wait_ge(s["qe"], 2 * j + 1)
                project(prb[0][:, :], a, slice(2 * P, 3 * P), n, "kp")

            def project_v(out, g, t):
                cols, rows = slice(g * S, (g + 1) * S), slice(t * P, (t + 1) * P)
                for i, (h, w) in enumerate(((vhi, wvhi), (vhi, wvlo), (vlo, wvhi))):
                    last = pe.matmul(out[:, :], h[:, rows], w[:, cols], start=(i == 0), stop=(i == 2))
                last.then_inc(s["vp"], 1)

            def scores(j, k):
                h, q = k // QT, ORDER[k % QT]
                if k % QT == 0:
                    pe.wait_ge(s["ql"], 2 * j + h + 1)
                    pe.wait_ge(s["kl"], 2 * j + h + 1)
                wait(pe, "tt", 8 * j + k - 1)
                out = scb[k % 2][:, 0:P * (q + 1)]
                if q == 0:
                    last = pe.matmul(out, qx[:, h, 0:P], kx[:, h, :], start=True, stop=True)
                else:
                    for i, (a, b) in enumerate(((qhi, khi), (qhi, klo), (qlo, khi))):
                        last = pe.matmul(out, a[:, h, (q - 1) * P:q * P], b[:, h, 0:P * (q + 1)],
                                         start=(i == 0), stop=(i == 2))
                last.then_inc(s["sc"], 1)

            def transpose_group(out, j, par, h, g):
                if g == 0:
                    pe.wait_ge(s["nm"], 2 * j + h + 1)
                for n, (q, k) in enumerate(GROUPS[g]):
                    last = pe.transpose(out[:, n * P:(n + 1) * P],
                                        prob[:, par, h, QOFF[q] + k * P:QOFF[q] + (k + 1) * P], ident)
                last.then_inc(s["tr"], 1)

            def transposes(j, par, h, g):
                i = 3 * h + g
                if i >= 2:
                    n = i - 2
                    pe.wait_ge(s["evA" if n < 1 else "evB"], j + 1 if n < 1 else 5 * j + n)
                transpose_group(trb[i % 2], j, par, h, g)

            def weighted(j, a, ve, by_dve=1):
                pe.wait_ge(s["evA"], j + by_dve)
                pe.wait_ge(s["evB"], 5 * j + 6 - by_dve)
                pe.wait_ge(s["ve"], ve)
                wait(pe, "ol", j)
                g, at = a // 4, a % 4 * P
                for k in range(QT):
                    for h in range(2):
                        last = pe.matmul(otb[h * HD:(h + 1) * HD, k * P:S], v[:, g, k, at + h * HD:at + (h + 1) * HD],
                                         pt[:, h, KOFF[k]:KOFF[k] + S - k * P], start=(k == 0), stop=(k == QT - 1))
                last.then_inc(s["pv"], 1)

            def project_out(j, a):
                pe.wait_ge(s["ol"], j + 1)
                wait(pe, "ac", j)
                for i, (w, o) in enumerate(((wohi, ohi), (wohi, olo), (wolo, ohi))):
                    last = pe.matmul(opb[:, :], w[:, a, :], o[:, :], start=(i == 0), stop=(i == 2))
                last.then_inc(s["op"], 1)

            def turn_a(b):
                pe.wait_ge(s["ga"], b)
                for q in range(QT):
                    last = pe.transpose(opb[:, q * P:(q + 1) * P], hn[:, q * P:(q + 1) * P], ident)
                last.then_inc(s["t_a"], 1)

            def turn_h(b):
                pe.wait_ge(s["xh"], b)
                for q in range(QT):
                    last = pe.transpose(opb[:, q * P:(q + 1) * P], xh[:, q, :], ident)
                last.then_inc(s["t_h"], 1)

            def logits(b):
                pe.wait_ge(s["hh"], b)
                for q in range(QT):
                    last = pe.matmul(opb[:, q * E:(q + 1) * E], h2T[:, q * P:(q + 1) * P], wg[:, :],
                                     start=True, stop=True)
                last.then_inc(s["lg"], 1)

            def places(b):
                pe.wait_ge(s["oh"], b)
                pe.matmul(opb[:, 0:QT * E], upper16[:, :], oh16[:, :], start=True, stop=False)
                for t in range(1, QT):
                    pe.matmul(opb[:, t * E:QT * E], ones16[:, :], oh16[:, 0:(QT - t) * E],
                              start=False, stop=(t == QT - 1))
                for t in range(QT):
                    last = pe.matmul(opb[:, QT * E:(QT + 1) * E], ones16[:, :], oh16[:, t * E:(t + 1) * E],
                                     start=(t == 0), stop=(t == QT - 1))
                last.then_inc(s["pre"], 1)

            def turn(b, first, last):
                for a in range(PAIRS):
                    step(8 * b + a, a % 2, b, a, first, last)

            def step(j, par, b, a, first, last):
                before, after = not (first and a == 0), not (last and a == PAIRS - 1)
                n, m = (b, a + 1) if a + 1 < PAIRS else (b + 1, 0)
                for k in range(8):
                    scores(j, k)
                    if k == 4 and after:
                        project_q(j + 1, n, m, 0)
                    if before and k in TURN:
                        transposes(j - 1, 1 - par, *divmod(TURN.index(k), 3))
                    if k == 1 and not (last and V_OF[a][0]):
                        pe.wait_ge(s["qe"], 2 * j + 2)
                        if a == 5:
                            pe.wait_ge(s["vlo"], b + 2)
                        project_v(prb[1], *V_OF[a][1:])
                    if k == 2 and not (first and a < 2):
                        if a == 3 and not first:
                            pe.wait_ge(s["x2"], b)
                        if a == 4 and not last:
                            pe.wait_ge(s["hn"], b + 2)
                        if a in (5, 6, 7) and not first:
                            pe.wait_ge(s[("hh", "lge", "prx")[a - 5]], b)
                        project_out(j - 2, (a - 2) % PAIRS)
                    if k == 4:
                        if a == 2 and not first:
                            wait(pe, "ac", j - 1)
                            turn_a(b)
                        if a == 3 and not last:
                            wait(pe, "ac", j - 1)
                            turn_x(b + 1)
                        if a in (4, 5, 6) and not first:
                            wait(pe, "ac", j - 1)
                            (turn_h, logits, places)[a - 4](b)
                    if k == 5 and after:
                        project_k(j + 1, n, m)
                    if k == 7 and before:
                        weighted(j - 1, (a - 1) % PAIRS, 8 * b + 4 * ((a - 1) // 4) + 4)
                if after:
                    project_q(j + 1, n, m, 1, 8 * B if last and V_OF[a][0] else j + 4)

            pe.wait_ge(s["whi"], 5)
            pe.wait_ge(s["wlo"], 4)
            pe.wait_ge(s["wlo_k"], 1)
            project_q(0, None, 0, 0)
            project_q(0, None, 0, 1)
            project_k(0, None, 0)
            pe.wait_ge(s["wv"], 2)
            for t in range(3):
                project_v(bank[V_BANKS[t]], 0, t)
            pe.wait_ge(s["wos"], 2)
            pe.wait_ge(s["mev"], 1)
            pe.wait_ge(s["bias"], 4)
            pe.wait_ge(s["misc"], 48)
            pe.wait_ge(s["ve"], 3)
            pe.wait_ge(s["ktab"], 48)
            pe.wait_ge(s["kt"], 4)
            batches(pe, turn)
            for i in range(6):
                transpose_group(free[i], NJ - 1, 1, *divmod(i, 3))
            project_out(NJ - 2, PAIRS - 2)
            weighted(NJ - 1, PAIRS - 1, NJ, 3)
            project_out(NJ - 1, PAIRS - 1)
            pe.wait_ge(s["ac"], NJ)
            turn_a(B)
            pe.wait_ge(s["x2"], B)
            turn_h(B)
            logits(B)
            pe.wait_ge(s["lge"], B)
            places(B)

            def turn_e(r):
                for t in range(ST):
                    last = pe.transpose(bank[r % 2][:, t * P:(t + 1) * P], slots[:, r % 4, t, 0:D], ident)
                last.then_inc(s["tx"], 1)

            def hidden(e, r):
                pe.wait_ge(s["w1l"], e + 1)
                pe.wait_ge(s["xl"], e + 1)
                par = r % 2
                for n in range(NB):
                    for i, (w, x_) in enumerate(((w1hi, xhi), (w1lo, xhi), (w1hi, xlo))):
                        last = pe.matmul(bank[2 + n][:, 0:CAP], w[:, par, n, :], x_[:, par, :],
                                         start=(i == 0), stop=(i == 2))
                    last.then_inc(s["hm"], 1)

            def down(e, r):
                pe.wait_ge(s["hh2"], 2 * e + 1)
                for t in range(ST):
                    for n in range(NB):
                        if t == 0:
                            pe.wait_ge(s["hr" if n % 2 == 0 else "hh2"], 2 * e + n // 2 + 1)
                        last = pe.matmul(bank[6 + r % 2][:, t * P:(t + 1) * P], hid[:, r % 2, n, t * P:(t + 1) * P],
                                         w2[:, r, n, :], start=(n == 0), stop=(n == NB - 1))
                last.then_inc(s["ym"], 1)

            pe.wait_ge(s["prx"], B)
            pe.wait_ge(s["xl0"], 16)
            turn_e(0)
            with pe.Fori(0, E // 8) as g:
                for r in range(8):
                    e = 8 * g + r
                    pe.wait_ge(s[f"w{r}"], 32 * (g + 1))
                    hidden(e, r)
                    pe.wait_ge(s[f"xl{(r + 1) % 4}"], 32 * g + 16 * ((r + 1) // 4) + 16)
                    turn_e(r + 1)
                    down(e, r)

        @block.vector
        def _(dve):
            link = Chain(dve, s["dch"])
            link(dve.memset(fill[:, :], 0.0))
            dve.memset(fill[:, RW - 1:RW], float(NOWHERE)).then_inc(s["zero"], 1)
            dve.memset(ones16[:, :], 1.0).then_inc(s["zero"], 1)
            dve.memset(base[:, :], 0.0).then_inc(s["zero"], 1)
            dve.wait_ge(s["t_small"], 1)
            dve.tensor_copy(smallT[:, :], bank[0][:, 0:80]).then_inc(s["smallT"], 1)
            dve.wait_ge(s["t_pos"], 1)
            dve.wait_ge(s["posT"], 1)
            for h in range(2):
                rows = slice(h * HD, (h + 1) * HD)
                dve.tensor_copy(posT[rows, :, h, :, :], bank[1][rows, 0:PAIRS * FREQS]
                                .rearrange("p (a o f) -> p a o f", o=1, f=FREQS).to_broadcast([HD, PAIRS, 2, FREQS]))\
                    .then_inc(s["posT"], 1)
            wqT = prob[:, 0, :, :].rearrange("p a w -> p (a w)")
            for i in range(2):
                dve.wait_ge(s["t_wq"], i + 1)
                dve.tensor_copy(wqT[:, i * 512:(i + 1) * 512], bank[2 + i][:, :]).then_inc(s["wqT"], 1)

            dve.wait_ge(s["e_silu"], 1)
            link(dve.tensor_scalar(silu[:, 1, :], silu[:, 0, :], 1.0, None, ALU.add))
            link(dve.reciprocal(silu[:, 2, :], silu[:, 1, :]))
            dve.tensor_tensor(silu[:, 3, :], silu[:, 2, :], smallT[:, 8:16], ALU.mult).then_inc(s["silu"], 1)

            def moments(i):
                st, m = stats[:, i], mom[:, i]
                me, mo, ve, vo = (st[:, :, c] for c in (1, 4, 2, 5))
                yield lambda: (link(dve.tensor_tensor(m[:, 0, :], me, mo, ALU.add)),
                               link(dve.tensor_tensor(m[:, 1, :], me, mo, ALU.subtract)),
                               link(dve.tensor_tensor(m[:, 2, :], ve, vo, ALU.add)))
                yield lambda: (link(dve.tensor_tensor(m[:, 3, :], m[:, 1, :], m[:, 1, :], ALU.mult)),
                               link(dve.scalar_tensor_tensor(m[:, 1, :], m[:, 3, :], D / 4.0, m[:, 2, :],
                                                             ALU.mult, ALU.add)))
                yield lambda: (link(dve.tensor_scalar(m[:, 0, :], m[:, 0, :], 0.5, None, ALU.mult)),
                               dve.tensor_scalar(m[:, 4, :], m[:, 1, :], 1.0 / D, EPS, ALU.mult, ALU.add)
                               .then_inc(s[f"rst{i + 1}"], 1))

            def x_of(n, q):
                return x[:, bass.ds(n * QT + q, 1), :].rearrange("p a d -> p (a d)")

            def stats1(n):
                for q in range(QT):
                    end = dve.bn_stats(stats[:, 0, q, :], x_of(n, q))
                link(end)

            def xhat1(n):
                dve.wait_ge(s["rs1"], n + 1)
                for q in range(QT):
                    end = dve.tensor_scalar(xn[:, q, :], x_of(n, q), mom[:, 0, 0, q:q + 1], mom[:, 0, 5, q:q + 1],
                                            ALU.subtract, ALU.mult)
                end.then_inc(s["xn"], 1)

            def low(n):
                dve.wait_ge(s["vhi"], n + 1)
                dve.tensor_tensor(vlo[:, :], hn[:, :], vhi[:, :], ALU.subtract).then_inc(s["vlo"], 1)

            dve.wait_ge(s["x0"], 16)
            stats1(0)
            for part in moments(0):
                part()
            dve.wait_ge(s["wv"], 1)
            dve.tensor_tensor(wvlo[:, :], qkv[:, 2, :], wvhi[:, :], ALU.subtract).then_inc(s["wv"], 1)
            xhat1(0)
            dve.wait_ge(s["mod_mm"], 1)
            half = lambda c: bank[0][:, c * B:(c + 2) * B].rearrange("p (i b) -> p i b", i=2)
            dve.tensor_copy(modT[:, 0:3:2, :], half(0)).then_inc(s["modT"], 1)
            link(dve.tensor_copy(modT[:, 4, :], bank[0][:, 4 * B:5 * B]))
            dve.tensor_scalar(modT[:, 1:4:2, :], half(2), 1.0, None, ALU.add).then_inc(s["modT"], 1)
            dve.wait_ge(s["whi"], 2)
            for h in range(2):
                cols = slice(h * P, h * P + HD)
                dve.tensor_tensor(wlo[:, :, cols], qkv[:, 0, :].rearrange("p (a h d) -> p a h d", h=2, d=HD)[:, :, h, :],
                                  whi[:, :, cols], ALU.subtract).then_inc(s["wlo"], 1)
            for i in range(2):
                dve.wait_ge(s["whi"], 4 + i)
                dve.tensor_tensor(g_of(wlo, i), bank[4 + i][:, :].rearrange("p (a h w) -> p a h w", h=2, w=HD),
                                  g_of(whi, i), ALU.subtract).then_inc(s["wlo"], 1)
            low(0)
            dve.wait_ge(s["vlo"], 1)
            dve.tensor_copy(hlo[:, 0, :], vlo[:, :]).then_inc(s["hld"], 1)
            dve.tensor_copy(mrow[:, :, :].rearrange("p a d -> p (a d)"), bank[6][0:B, 0:3 * D]).then_inc(s["mev"], 1)

            def scores(j, par, k):
                q = ORDER[k % QT]
                w = P * (q + 1)
                waits(dve, ("consts", 16), ("sc", 8 * j + k + 1), ("ex", 8 * j + k - 3))
                dve.tensor_tensor_reduce(out=srow[:, k % 4, 0:w], in0=scb[k % 2][:, 0:w], in1=mask[:, S - w:S],
                                         scale=-1.0, scalar=BIG, op0=ALU.add, op1=ALU.min,
                                         accum_out=nmax[:, par, k:k + 1]).then_inc(s["tt"], 1)

            def evac_pt(j, i=0, source=trb[0]):
                dve.wait_ge(s["tr"], 6 * j + i + 1)
                h, g = divmod(i, 3)
                dve.tensor_copy(pt[:, h, KOFF[g]:KOFF[g] + GW[g]], source[:, 0:GW[g]]).then_inc(s["evA"], 1)

            def recip(j, par, h):
                dve.wait_ge(s["ex"], 8 * j + 4 * h + 4)
                dve.reciprocal(rsum[:, par, 4 * h:4 * h + 4], sums[:, par, 4 * h:4 * h + 4]).then_inc(s["rc"], 1)

            def evac_q(j, a, h):
                dve.wait_ge(s["qp"], 2 * j + h + 1)
                dve.scalar_tensor_tensor(qx[:, h, :], prb[h][:, :], qbias[:, h, a:a + 1], qtab,
                                         ALU.add, ALU.mult).then_inc(s["qe"], 1)

            def low_k(j, h):
                dve.wait_ge(s["ke"], 2 * j + h + 1)
                dve.scalar_tensor_tensor(klo[0:HD, h, :], prb[0][h * HD:(h + 1) * HD, :], C_QKV, khi[0:HD, h, :],
                                         ALU.mult, ALU.subtract).then_inc(s["kl"], 1)

            def accumulate(j, a):
                dve.wait_ge(s["op"], j + 1)
                wait(dve, "ac", j)
                if a == 0:
                    dve.tensor_scalar(acc[:, :], opb[:, :], bo[:, 0:1], None, ALU.add).then_inc(s["ac"], 1)
                else:
                    dve.tensor_tensor(acc[:, :], opb[:, :], acc[:, :], ALU.add).then_inc(s["ac"], 1)

            def low_o(j):
                dve.wait_ge(s["oe"], j + 1)
                dve.scalar_tensor_tensor(olo[:, :], otb[:, :], C_QKV * C_OUT, ohi[:, :], ALU.mult, ALU.subtract)\
                    .then_inc(s["ol"], 1)

            def residual(b):
                dve.wait_ge(s["vhi"], b + 1 if not isinstance(b, int) or b < B else B)
                dve.wait_ge(s["gates"], 2)
                dve.wait_ge(s["ac"], 8 * b)
                dve.tensor_scalar(hn[:, :], acc[:, :], modT[:, 4, bass.ds(b - 1, 1)], None, ALU.mult)\
                    .then_inc(s["ga"], 1)

            def residual2(b):
                dve.wait_ge(s["t_a"], b)
                if isinstance(b, int):
                    dve.wait_ge(s["scat"], 64 * (b - 1))
                else:
                    dve.wait_ge(s["nm"], 16 * b)
                dve.tensor_tensor(row[:, :, D:2 * D], x[:, bass.ds((b - 1) * QT, QT), :],
                                  opb[:, :].rearrange("p (t d) -> p t d", t=QT), ALU.add)\
                    .then_inc(s["x2"], 1)

            def stats2(b):
                dve.wait_ge(s["x2"], b)
                for q in range(QT):
                    end = dve.bn_stats(stats[:, 1, q, :], row[:, q, D:2 * D])
                link(end)

            def xhat2(b):
                dve.wait_ge(s["rs2"], b)
                if not isinstance(b, int) or b < B - 1:
                    dve.wait_ge(s["t_x"], b + 2)
                for q in range(QT):
                    end = dve.tensor_scalar(xh[:, q, :], row[:, q, D:2 * D], mom[:, 1, 0, q:q + 1],
                                            mom[:, 1, 5, q:q + 1], ALU.subtract, ALU.mult)
                end.then_inc(s["xh"], 1)

            te = lambda t: t.rearrange("p (t e) -> p t e", e=E)
            each = lambda t: t[:, :, None].to_broadcast([P, QT, E])
            lmax, esum, gate, emax, where, late, tmp1, tmp2 = (rsm[:, i, :] for i in range(8))

            def gating(b):
                dve.wait_ge(s["lg"], b)
                dve.tensor_tensor(te(lgt[:, 0, :]), te(opb[:, 0:QT * E]), bg[:, None, :].to_broadcast([P, QT, E]),
                                  ALU.add).then_inc(s["lge"], 1)
                dve.wait_ge(s["lge"], b)
                link(dve.tensor_reduce(lmax, te(lgt[:, 0, :]), AX.X, ALU.max))
                dve.tensor_tensor(te(lgt[:, 1, :]), te(lgt[:, 0, :]), each(lmax), ALU.subtract).then_inc(s["lm"], 1)

            def choice(b):
                dve.wait_ge(s["lm"], b)
                link(dve.scalar_tensor_tensor(te(lgt[:, 3, :]), te(lgt[:, 1, :]), 0.0,
                                              desc[:, None, :].to_broadcast([P, QT, E]), ALU.is_ge, ALU.mult))
                link(dve.tensor_reduce(emax, te(lgt[:, 3, :]), AX.X, ALU.max))
                dve.tensor_tensor(te(oh16[:, :]), te(lgt[:, 3, :]), each(emax), ALU.is_equal).then_inc(s["oh"], 1)

            def gate_of(b):
                dve.wait_ge(s["lex"], b)
                link(dve.tensor_reduce(esum, te(lgt[:, 2, :]), AX.X, ALU.add))
                dve.reciprocal(gate, esum).then_inc(s["gate"], 1)

            def place(b):
                dve.wait_ge(s["pre"], b)
                link(dve.tensor_tensor(te(lgt[:, 0, :]), te(opb[:, 0:QT * E]),
                                       base[:, None, :].to_broadcast([P, QT, E]), ALU.add))
                dve.tensor_tensor(base[:, :], base[:, :], opb[:, QT * E:(QT + 1) * E], ALU.add).then_inc(s["prx"], 1)
                dve.wait_ge(s["prx"], b)
                link(dve.tensor_tensor(lgt[:, 0, :], lgt[:, 0, :], oh16[:, :], ALU.mult))
                link(dve.tensor_reduce(where, te(lgt[:, 0, :]), AX.X, ALU.add))

            def route(b):
                link(dve.tensor_scalar(late, where, float(CAP), float(NOWHERE), ALU.is_ge, ALU.mult))
                link(dve.scalar_tensor_tensor(tmp1, emax, -float(CAP), where, ALU.mult, ALU.add))
                link(dve.scalar_tensor_tensor(tmp2, tmp1, float(E * CAP), late, ALU.add, ALU.add))

            def index(b):
                link(dve.tensor_copy(sidx[:, :], tmp2))
                dve.tensor_copy(row[:, :, 3 * D:RW], token[:, bass.ds((b - 1) * QT, QT)][:, :, None])\
                    .then_inc(s["idx"], 1)

            def modulation():
                dve.wait_ge(s["mev"], 1)
                dve.tensor_copy(upper16[:, :], upper).then_inc(s["zero"], 1)
                link(dve.tensor_scalar(mrow[:, 1, :], mrow[:, 1, :], 1.0, None, ALU.add))
                for g_, sign, size in ((modT[:, 4, :], gtmp[:, 0, :], gtmp[:, 1, :]),
                                       (mrow[:, 2, :], mtmp[:, 0, :], mtmp[:, 1, :])):
                    link(dve.tensor_scalar(sign, g_, 0.0, 2.0, ALU.is_ge, ALU.mult))
                    link(dve.scalar_tensor_tensor(size, sign, -1.0, g_, ALU.add, ALU.mult))
                    link(dve.tensor_scalar(size, size, 0.25, None, ALU.max))
                    dve.scalar_tensor_tensor(g_, sign, -1.0, size, ALU.add, ALU.mult).then_inc(s["gates"], 1)

            def extra(b, first, last):
                parts = {a: [] for a in range(PAIRS)}
                if not last:
                    n = b + 1
                    parts[0] = [lambda: stats1(n), *moments(0)]
                    parts[2] = [lambda: xhat1(n)]
                    parts[4] = [lambda: low(n)]
                if not first:
                    parts[1] = [None, lambda: residual(b)]
                    parts[2] = [lambda: residual2(b), lambda: stats2(b), *parts[2], *moments(1)]
                    parts[3] = [None, lambda: xhat2(b)]
                    parts[5] = [lambda: gating(b), lambda: choice(b), None, lambda: gate_of(b)]
                    parts[6] = [lambda: place(b), lambda: route(b), lambda: index(b)]
                else:
                    parts[1] = [modulation]
                return parts

            def turn(b, first, last):
                parts = extra(b, first, last)
                for a in range(PAIRS):
                    step(8 * b + a, a % 2, a, first, last, parts[a])

            def step(j, par, a, first, last, parts):
                before, after = not (first and a == 0), not (last and a == PAIRS - 1)
                for k in range(8):
                    scores(j, par, k)
                    if before and k == 0:
                        evac_pt(j - 1)
                    if k == 0 and not (first and a < 2):
                        low_o(j - 2)
                    if k == KLO:
                        low_k(j, 1)
                    if k == 3 and not (first and a < 2):
                        accumulate(j - 2, (a - 2) % PAIRS)
                    if k == 4:
                        recip(j, par, 0)
                        if after:
                            evac_q(j + 1, (a + 1) % PAIRS, 0)
                    if k >= 5 and parts:
                        part = parts.pop(0)
                        if part:
                            part()
                if after:
                    low_k(j + 1, 0)
                recip(j, par, 1)
                if after:
                    evac_q(j + 1, (a + 1) % PAIRS, 1)
                for part in parts:
                    if part:
                        part()

            dve.wait_ge(s["misc"], 48)
            dve.wait_ge(s["bias"], 4)
            dve.wait_ge(s["x1"], 16)
            evac_q(0, 0, 0)
            evac_q(0, 0, 1)
            low_k(0, 0)
            dve.wait_ge(s["wos"], 1)
            dve.tensor_tensor(wolo[:, :, :], wo, wohi[:, :, :], ALU.subtract).then_inc(s["wos"], 1)
            batches(dve, turn, lambda i: link.enter(i, LINKS), link.leave)
            low_o(NJ - 2)
            for i in (0, 2, 4):
                evac_pt(NJ - 1, i, free[i])
            accumulate(NJ - 2, PAIRS - 2)
            low_o(NJ - 1)
            accumulate(NJ - 1, PAIRS - 1)
            for part in (residual, residual2, stats2):
                part(B)
            for part in moments(1):
                part()
            for part in (xhat2, gating, choice, gate_of, place, route, index):
                part(B)

            def low_w1(e, par):
                slot = e & 7 if isinstance(e, int) else dve.compute_val(e & 7)
                dve.wait_ge(s["w1h"], e + 1)
                dve.tensor_tensor(w1lo[:, par, :, :].rearrange("p n d -> p (n d)"),
                                  w1[:, bass.ds(slot, 1), :, :].rearrange("p r n d -> p (r n d)"),
                                  w1hi[:, par, :, :].rearrange("p n d -> p (n d)"), ALU.subtract)\
                    .then_inc(s["w1l"], 1)

            def low_x(e, par):
                dve.wait_ge(s["xt"], e + 1)
                dve.tensor_tensor(xlo[:, par, :], bank[par][:, 0:CAP], xhi[:, par, :], ALU.subtract)\
                    .then_inc(s["xl"], 1)

            def relu(e, par):
                for n in range(1, NB, 2):
                    dve.wait_ge(s["hm"], NB * e + n + 1)
                    dve.tensor_scalar(hid[:, par, n, :], bank[2 + n][:, 0:CAP], smallT[:, bass.ds(16 + NB * e + n, 1)],
                                      0.0, ALU.add, ALU.max).then_inc(s["hh2"], 1)

            def output(e, r, first=False):
                par = r % 2
                if not first:
                    dve.wait_ge(s[f"ysc{par}"], 16 * (e - par))
                dve.tensor_copy(yidx[:, par, :], slots[:, r, :, 3 * D]).then_inc(s["yi"], 1)
                dve.wait_ge(s["ym"], e + 1)
                rows = ye[:, par, :, :]
                link(dve.tensor_tensor(rows, bank[6 + par][:, 0:CAP].rearrange("p (t d) -> p t d", t=ST),
                                       one(b2, e, slice(None)).to_broadcast([P, ST, D]), ALU.add))
                link(dve.tensor_tensor(rows, rows, slots[:, r, :, 2 * D:3 * D], ALU.mult))
                dve.tensor_tensor(rows, rows, slots[:, r, :, D:2 * D], ALU.add).then_inc(s["y"], 1)

            dve.wait_ge(s["scat"], 64 * B)
            dve.wait_ge(s["b2"], 16)
            for e in range(2):
                low_w1(e, e)
            low_x(0, 0)

            def expert(e, r, first=False):
                par = r % 2
                relu(e, par)
                low_x(e + 1, 1 - par)
                if not isinstance(e, int) or e:
                    output(e - 1, (r - 1) % 4, first)
                low_w1(e + 2, par)

            for e in range(4):
                expert(e, e, e < 3)
            with dve.Fori(1, E // 4) as g:
                link.enter(g - 1, 8)
                for r in range(4):
                    expert(4 * g + r, r)
            link.leave(E // 4 - 1)
            output(E - 1, 3)


def host_constants():
    k = np.arange(S, dtype=np.float64)
    f = np.arange(FREQS)
    inv = 1250.0 ** (-(f // 2 * 2) / FREQS)
    ang = inv[:, None] * k[None, :]
    even = (f % 2 == 0)[:, None]
    sig = np.sqrt(2.0) * FREQS ** -0.5
    cq = C_QKV * HD ** -0.5
    qtab = np.concatenate([np.full((HD, S), cq),
                           cq * sig * np.where(even, np.sin(ang), np.cos(ang)),
                           cq * sig * np.where(even, -np.cos(ang), np.sin(ang))])
    ktab = np.concatenate([np.cos(ang), np.sin(ang)])
    causal = np.where(np.arange(P)[None, :] > np.arange(P)[:, None], NEG, 0.0)
    mask = np.concatenate([np.zeros((P, S - P)), causal], axis=1)
    desc = np.broadcast_to(E - np.arange(E), (P, E))
    upper = (np.arange(P)[:, None] < np.arange(P)[None, :]).astype(np.float64)
    token = (np.arange(P)[:, None] + P * np.arange(TILES)[None, :]).astype(np.float64)
    consts = np.concatenate([np.eye(P), mask, qtab, desc, upper, token], axis=1)
    return np.ascontiguousarray(consts, dtype=np.float32), np.ascontiguousarray(ktab, dtype=np.float32)


NAMES = ["L0_attn_input", "L0_attn_qkv", "L0_attn_q_bias", "L0_attn_positional", "L0_attn_out_kernel",
         "L0_attn_out_bias", "L0_ffn_Wg", "L0_ffn_bg", "L0_ffn_W1", "L0_ffn_b1", "L0_ffn_W2", "L0_ffn_b2",
         "L0_c", "L0_wmod"]


def kernel(**inputs):
    import concourse.bacc as bacc
    from concourse.bass_utils import run_bass_kernel_spmd

    nc = bacc.Bacc("TRN2", target_bir_lowering=False, num_devices=1)
    arrays, args = {}, []
    consts, ktab = host_constants()
    for name, a in [(n, np.ascontiguousarray(inputs[n])) for n in NAMES] + [("consts", consts), ("ktab", ktab)]:
        arrays[f"in_{name}"] = a
        args.append(nc.dram_tensor(f"in_{name}", a.shape, mybir.dt.from_np(a.dtype), kind="ExternalInput").ap())
    out = nc.dram_tensor("out_0", (B, S, D), F32, kind="ExternalOutput").ap()
    program(nc, *args, out)
    r = run_bass_kernel_spmd(nc, [arrays], core_ids=[0])
    return r.results[0]["out_0"]
```
